# Optimizing a Trainium2 kernel written in Bass

```python
import numpy as np
import jax
import jax.numpy as jnp

def _softmax(x, axis=-1):
    return jax.nn.softmax(x, axis=axis)

def _gelu(x):
    return jax.nn.gelu(x, approximate=True)

def _silu(x):
    return jax.nn.silu(x)

def _sigmoid(x):
    return jax.nn.sigmoid(x)

def _layernorm(x, axis=-1, eps=1e-05):
    m = jnp.mean(x, axis=axis, keepdims=True)
    v = jnp.var(x, axis=axis, keepdims=True)
    return (x - m) / jnp.sqrt(v + eps)

def _scatter_add(tgt, idx, src, axis=0):
    return tgt.at[idx].add(src)

def _segment_sum(src, seg, n):
    return jax.ops.segment_sum(src, seg, n)
kernel_name = 'mk_audio_tower_d1_tok_audfeat512_r4_d1231c'

def setup_inputs(seed: int=0):
    np.random.seed(seed)
    _w = jnp.asarray

    def _rec_inputs():
        import jax
        import jax.numpy as jnp
        _rk = jax.random.key(seed)
        x = -0.000125008 + 0.999885 * jax.random.normal(jax.random.fold_in(_rk, 1), (32, 256, 128), jnp.float32)
        return x
    x = _rec_inputs()

    def _L0_tok_setup():
        import jax, jax.numpy as jnp
        import numpy as np
        OFFSETS = np.array([-2, -1, 0, 1, 2], dtype=np.int32)
        STRIDE = 1

        def _valid_window_indices(T):
            t = np.arange(0, T, STRIDE, dtype=np.int32)
            idx = t[:, None] + OFFSETS[None, :]
            valid = np.all((idx >= 0) & (idx < T), axis=1)
            return jnp.asarray(idx[valid])
        key = jax.random.key(seed)
        kx, kw = jax.random.split(key)
        B, T, F, K, U = (32, 512, 128, len(OFFSETS), 128)
        x = jax.random.normal(kx, (B, T, F), dtype=jnp.float32)
        W = jax.random.normal(kw, (K * F, U), dtype=jnp.float32) * (1.0 / np.sqrt(K * F))
        b = jnp.zeros((U,), dtype=jnp.float32)
        return {'x': x, 'W': W, 'b': b}
    _L0_tok_all = _L0_tok_setup()
    _L0_tok_in = {k: v for k, v in _L0_tok_all.items() if k in ('W', 'b')}
    del _L0_tok_all

    def _L0_attn_setup():
        import jax, jax.numpy as jnp
        import numpy as np
        EPS = 1e-05
        key = jax.random.key(seed)
        ks = jax.random.split(key, 5)
        B, T, D = (2, 1024, 128)
        x = jax.random.normal(ks[0], (B, T, D), dtype=jnp.float32)
        w_qkv = jax.random.normal(ks[1], (D, 3 * D), dtype=jnp.float32) * (1.0 / np.sqrt(D))
        w_out = jax.random.normal(ks[2], (D, D), dtype=jnp.float32) * (1.0 / np.sqrt(D))
        b_out = jnp.zeros((D,), dtype=jnp.float32)
        gamma = jnp.ones((D,), dtype=jnp.float32)
        beta = jnp.zeros((D,), dtype=jnp.float32)
        return {'x': x, 'w_qkv': w_qkv, 'w_out': w_out, 'b_out': b_out, 'gamma': gamma, 'beta': beta}
    _L0_attn_all = _L0_attn_setup()
    _L0_attn_in = {k: v for k, v in _L0_attn_all.items() if k in ('w_qkv', 'w_out', 'b_out', 'gamma', 'beta')}
    del _L0_attn_all

    def _L0_ffn_setup():
        import jax, jax.numpy as jnp
        import numpy as np
        B, S, H, E, F = (4, 512, 128, 8, 128)
        key = jax.random.key(seed)
        k = jax.random.split(key, 7)
        x = jax.random.normal(k[0], (B, S, H), dtype=jnp.float32)
        Wr = jax.random.normal(k[1], (H, E), dtype=jnp.float32) / np.sqrt(H)
        br = jnp.zeros((E,), dtype=jnp.float32)
        W1 = jax.random.normal(k[2], (E, H, F), dtype=jnp.float32) / np.sqrt(H)
        b1 = jnp.zeros((E, F), dtype=jnp.float32)
        W2 = jax.random.normal(k[3], (E, F, H), dtype=jnp.float32) / np.sqrt(F)
        b2 = jnp.zeros((E, H), dtype=jnp.float32)
        return {'x': x, 'Wr': Wr, 'br': br, 'W1': W1, 'b1': b1, 'W2': W2, 'b2': b2}
    _L0_ffn_all = _L0_ffn_setup()
    _L0_ffn_in = {k: v for k, v in _L0_ffn_all.items() if k in ('Wr', 'br', 'W1', 'b1', 'W2', 'b2')}
    del _L0_ffn_all
    return {'x': x, 'L0_tok_W': _L0_tok_in['W'], 'L0_tok_b': _L0_tok_in['b'], 'L0_attn_w_qkv': _L0_attn_in['w_qkv'], 'L0_attn_w_out': _L0_attn_in['w_out'], 'L0_attn_b_out': _L0_attn_in['b_out'], 'L0_attn_gamma': _L0_attn_in['gamma'], 'L0_attn_beta': _L0_attn_in['beta'], 'L0_ffn_Wr': _L0_ffn_in['Wr'], 'L0_ffn_br': _L0_ffn_in['br'], 'L0_ffn_W1': _L0_ffn_in['W1'], 'L0_ffn_b1': _L0_ffn_in['b1'], 'L0_ffn_W2': _L0_ffn_in['W2'], 'L0_ffn_b2': _L0_ffn_in['b2']}

def reference(x, L0_tok_W, L0_tok_b, L0_attn_w_qkv, L0_attn_w_out, L0_attn_b_out, L0_attn_gamma, L0_attn_beta, L0_ffn_Wr, L0_ffn_br, L0_ffn_W1, L0_ffn_b1, L0_ffn_W2, L0_ffn_b2):
    import jax
    import jax.numpy as jnp

    def _L0_tok_ref(x, W, b):
        import jax, jax.numpy as jnp
        import numpy as np
        OFFSETS = np.array([-2, -1, 0, 1, 2], dtype=np.int32)
        STRIDE = 1

        def _valid_window_indices(T):
            t = np.arange(0, T, STRIDE, dtype=np.int32)
            idx = t[:, None] + OFFSETS[None, :]
            valid = np.all((idx >= 0) & (idx < T), axis=1)
            return jnp.asarray(idx[valid])
        B, T, F = x.shape
        idx = _valid_window_indices(T)
        win = x[:, idx, :]
        Tp, K = idx.shape
        win = win.reshape(B, Tp, K * F)
        return jnp.einsum('btd,du->btu', win, W) + b

    def _L0_attn_ref(x, w_qkv, w_out, b_out, gamma, beta):
        import jax, jax.numpy as jnp
        import numpy as np
        EPS = 1e-05
        B, T, D = x.shape
        H = 8
        hd = D // H
        scale = 1.0 / jnp.sqrt(jnp.asarray(hd, x.dtype))
        residual = x
        mu = jnp.mean(x, axis=-1, keepdims=True)
        var = jnp.mean((x - mu) ** 2, axis=-1, keepdims=True)
        xn = (x - mu) / jnp.sqrt(var + EPS) * gamma + beta
        qkv = (xn @ w_qkv).reshape(B, T, 3, H, hd)
        q, k, v = (qkv[:, :, 0], qkv[:, :, 1], qkv[:, :, 2])
        attn = jnp.einsum('bthd,bshd->bhts', q, k) * scale
        causal = jnp.triu(jnp.ones((T, T), dtype=bool), k=1)
        attn = jnp.where(causal[None, None], -jnp.inf, attn)
        attn = jax.nn.softmax(attn, axis=-1)
        out = jnp.einsum('bhts,bshd->bthd', attn, v).reshape(B, T, D)
        out = out @ w_out + b_out
        return out + residual

    def _L0_ffn_ref(x, Wr, br, W1, b1, W2, b2):
        import jax, jax.numpy as jnp
        import numpy as np
        B, S, H, E, F = (4, 512, 128, 8, 128)
        b, s, h = x.shape
        xt = x.reshape(-1, h)
        logits = xt @ Wr + br
        probs = jax.nn.softmax(logits, axis=-1)
        G = jnp.max(probs, axis=-1)
        idx = jnp.argmax(probs, axis=-1)
        h1 = jax.nn.relu(jnp.einsum('nh,ehf->nef', xt, W1) + b1)
        eo = jnp.einsum('nef,efh->neh', h1, W2) + b2
        Eout = jnp.take_along_axis(eo, idx[:, None, None], axis=1)[:, 0, :]
        y = G[:, None] * Eout
        return y.reshape(b, s, h)
    h = _L0_tok_ref(x, L0_tok_W, L0_tok_b)
    h = h + _L0_attn_ref(_layernorm(h, axis=-1), L0_attn_w_qkv, L0_attn_w_out, L0_attn_b_out, L0_attn_gamma, L0_attn_beta)
    h = h + _L0_ffn_ref(_layernorm(h, axis=-1), L0_ffn_Wr, L0_ffn_br, L0_ffn_W1, L0_ffn_b1, L0_ffn_W2, L0_ffn_b2)
    return h

_drawn_inputs = setup_inputs


def setup_inputs(seed=0):
    import zlib

    import numpy as np

    out = dict(_drawn_inputs(seed))
    spreads = {'L0_tok_b': (0.0, 0.1),
     'L0_attn_b_out': (0.0, 0.1),
     'L0_attn_gamma': (1.0, 0.2),
     'L0_attn_beta': (0.0, 0.1),
     'L0_ffn_br': (0.0, 0.1),
     'L0_ffn_b1': (0.0, 0.569),
     'L0_ffn_b2': (0.0, 0.415)}
    factors = {}
    for name, (base, spread) in spreads.items():
        noise = np.random.default_rng([zlib.crc32(name.encode()), seed]).standard_normal(out[name].shape)
        drawn = base * np.exp(spread * noise) if base else spread * noise
        out[name] = jnp.asarray(drawn.astype(out[name].dtype))
    for name, factor in factors.items():
        out[name] = (out[name] * factor).astype(out[name].dtype)
    return out
```

```python
from contextlib import ExitStack

import concourse.bass as bass
from concourse import mybir

F32 = mybir.dt.float32
BF16 = mybir.dt.bfloat16
I32 = mybir.dt.int32
ALU = mybir.AluOpType
ACT = mybir.ActivationFunctionType
AX = mybir.AxisListType

EPS = 1e-5
HEADS = 8
NEG = -1e30
UNROLL = 4


def build(nc, x, tok_w, tok_b, w_qkv, w_out, b_out, gamma, beta, w_r, b_r, w_1, b_1, w_2, b_2, out):
    NB, TIN, D = x.shape
    TAPS = tok_w.shape[0] // D
    T = TIN - TAPS + 1
    HALF = T // 2
    HD = D // HEADS
    E = w_r.shape[1]
    TOKENS = NB * T
    TRI = 3 * HALF
    REC = 2 * D + 2
    GATE, IDCOL = 2 * D, 2 * D + 1
    BIN = 64 * 128
    TILES = TOKENS // 128 + E - 1
    PAD_TILE = E * BIN // 128
    NO_TOKEN = 1 << 20
    PARTS = 3
    Q_SLOTS = [(0, (0, 1, 2)), (3, (0, 1)), (5, (0,))]
    K_SLOTS = [0, 0, 0, 1, 1, 2]
    ROWS = 6 * HD
    MROWS = ROWS + PARTS
    LAST = 6
    assert TOKENS % 128 == 0 and T % 2 == 0 and TOKENS + 128 <= BIN and D == 128 and E == 8

    bins = nc.dram_tensor("bins", [E * BIN + 128, REC], F32, kind="Internal").ap()
    splits = nc.dram_tensor("splits", [2, 2, PARTS, 128, T], BF16, kind="Internal").ap()

    with ExitStack() as ctx:
        def sb(name, shape, dt=F32):
            return ctx.enter_context(nc.sbuf_tensor(name, shape, dt))

        def sem(name):
            return ctx.enter_context(nc.semaphore(name))

        tok_w_sb = sb("tok_w_sb", [128, TAPS, D])
        w_qkv_sb = sb("w_qkv_sb", [128, 3 * D])
        w_out_sb = sb("w_out_sb", [128, D])
        gamma_sb = sb("gamma_sb", [128, 1])
        beta_sb = sb("beta_sb", [128, 1])
        tok_b_sb = sb("tok_b_sb", [128, D])
        b_out_sb = sb("b_out_sb", [1, D])
        w_r_sb = sb("w_r_sb", [128, E])
        b_r_sb = sb("b_r_sb", [E, 1])
        w_1_sb = sb("w_1_sb", [128, E * D])
        w_2_sb = sb("w_2_sb", [128, E * D])
        b_1_sb = sb("b_1_sb", [1, E * D])
        b_2_sb = sb("b_2_sb", [1, E * D])
        w_raw = sb("w_raw", [128, 2, D])
        w_q = sb("w_q", [128, D])
        w_k = sb("w_k", [128, D])
        w_v = sb("w_v", [128, D])
        gamma_q = sb("gamma_q", [128, 1])
        qk_bias = sb("qk_bias", [128, 2])
        v_bias = sb("v_bias", [128, 1])
        o_bias_row = sb("o_bias_row", [1, D])
        o_bias = sb("o_bias", [128, 2, D])
        ident = sb("ident", [128, 128])
        ident_bf = sb("ident_bf", [128, 128], BF16)
        causal = sb("causal", [128, 2, HALF], BF16)
        before = sb("before", [128, HALF], BF16)
        ones_bf = sb("ones_bf", [128, HALF], BF16)
        ones_row = sb("ones_row", [1, 128])
        neg_half = sb("neg_half", [128, 4])
        iota_i = sb("iota_i", [128, 2 * E], I32)
        bin_start = sb("bin_start", [128, E])
        rank_weight = sb("rank_weight", [128, E])
        token_i = sb("token_i", [128, 2], I32)
        token = sb("token", [128, 2])
        next_slot = sb("next_slot", [128, E])
        blank = sb("blank", [128, REC])

        xt = sb("xt", [128, 4, 2, D])
        xT = sb("xT", [128, 2, TIN])
        h = sb("h", [128, 2, 2, D])
        stats = sb("stats", [128, 2, 6])
        mv = sb("mv", [128, 2, 2, 2])
        var_e = sb("var_e", [128, 4])
        rstd = sb("rstd", [128, 2, 4])
        one_r = sb("one_r", [128, 2])
        neg_m = sb("neg_m", [128, 2])
        neg_mr = sb("neg_mr", [128, 2])
        base_h = sb("base_h", [128, 2, D])
        base = sb("base", [128, NB, 2, D])
        z = sb("z", [128, 2, 2, D])
        zT = sb("zT", [128, 2, T])
        qk = sb("qk", [128, 2, 2, T])
        rest = sb("rest", [128, 2, 2, T])
        parts = sb("parts", [128, 2, 2, PARTS, T], BF16)
        Q = sb("Q", [128, 4, HEADS, T], BF16)
        K = sb("K", [128, 4, HEADS, T], BF16)
        V = sb("V", [128, 4, 2, HEADS, 32])
        nmax3 = sb("nmax3", [128, 2, HEADS, 3])
        nmax = sb("nmax", [128, 2, HEADS])
        nmax_rest = sb("nmax_rest", [128, 2, HEADS])
        nmax_parts = sb("nmax_parts", [128, 2, 2, PARTS, HEADS], BF16)
        nmaxT = sb("nmaxT", [PARTS * HEADS, 2, T], BF16)
        P = sb("P", [128, HEADS, TRI])
        oT = sb("oT", [128, 2, T])
        rsum = sb("rsum", [128, 16])
        cn = sb("cn", [128, 2, 2, D])
        cT = sb("cT", [128, 2, T])
        rec = sb("rec", [128, 4, 2, REC])
        stats2 = sb("stats2", [128, 2, 6])
        mv2 = sb("mv2", [128, 2, 2, 2])
        var2_e = sb("var2_e", [128, 2])
        rstd2 = sb("rstd2", [128, 2, 2])
        z3T = sb("z3T", [128, 2, T])
        logitT = sb("logitT", [E, 2, T])
        lmax = sb("lmax", [128, 2])
        ldiff = sb("ldiff", [128, 2, 2, E])
        lexp = sb("lexp", [128, 2, 2, E])
        lsum = sb("lsum", [128, 2])
        hit = sb("hit", [128, 2, E])
        first = sb("first", [128, 2])
        onehot = sb("onehot", [128, 2, 2, E], BF16)
        pos = sb("pos", [128, 2, E])
        pos_own = sb("pos_own", [128, 2, E])
        slot_f = sb("slot_f", [128, 2])
        slot = sb("slot", [128, 4, 2], I32)

        RING = 8
        tile_in = sb("tile_in", [128, RING, REC])
        tT = sb("tT", [128, 2, 128])
        hid = sb("hid", [128, 2, D])
        hidT = sb("hidT", [128, 2, 128])
        y = sb("y", [128, 4, D])
        count = sb("count", [1, E])
        count_i = sb("count_i", [1, E], I32)
        tiles_i = sb("tiles_i", [1, E], I32)
        tiles_f = sb("tiles_f", [1, E])
        tiles_end = sb("tiles_end", [1, E])
        one_e = sb("one_e", [1, E])
        tile_no_i = sb("tile_no_i", [1, TILES], I32)
        tile_no = sb("tile_no", [1, TILES])
        passed = sb("passed", [1, TILES, E])
        skipped = sb("skipped", [1, TILES, E])
        expert_f = sb("expert_f", [1, TILES])
        start_f = sb("start_f", [1, TILES])
        row_f = sb("row_f", [1, TILES])
        row_a = sb("row_a", [1, TILES])
        row_b = sb("row_b", [1, TILES])
        expert_c = sb("expert_c", [1, TILES])
        row_i = sb("row_i", [1, TILES], I32)
        expert_i = sb("expert_i", [1, TILES], I32)
        tail_i = sb("tail_i", [1, E], I32)

        ps = ctx.enter_context(nc.psum_tensor("ps", [128, 8, 512], F32))
        NAT, TRN, AV, MID, M0, M1 = 0, 2, 4, 5, 6, 7

        loads = sem("loads")
        s_const = sem("s_const")
        s_chain = sem("s_chain")
        s_setup_pe = sem("s_setup_pe")
        s_setup = sem("s_setup")
        x_in = [sem(f"x_in{n}") for n in range(4)]
        xT_ps, xT_sb = sem("xT_ps"), sem("xT_sb")
        conv_ps, h_sb, st1, mv_sb = sem("conv_ps"), sem("h_sb"), sem("st1"), sem("mv_sb")
        pool_var, pool_rstd, pool_sc, base_part, base_sb = (sem(n) for n in ("pool_var", "pool_rstd", "pool_sc", "base_part", "base_sb"))
        z_sb, zT_ps, zT_sb = sem("z_sb"), sem("zT_ps"), sem("zT_sb")
        qk_ps, qk_sb, v_ps, v_sb = sem("qk_ps"), sem("qk_sb"), sem("v_ps"), sem("v_sb")
        part1, rest1, part2, part3 = sem("part1"), sem("rest1"), sem("part2"), sem("part3")
        split_out = [sem(f"split_out{n}") for n in range(2)]
        stack_in = [sem(f"stack_in{n}") for n in range(2)]
        nat_ps, max_sb = sem("nat_ps"), sem("max_sb")
        nm_sb, nmp1, nmr1, nmp2, nmp3 = (sem(n) for n in ("nm_sb", "nmp1", "nmr1", "nmp2", "nmp3"))
        nmT_ps, nmT_sb = sem("nmT_ps"), sem("nmT_sb")
        max_in = [sem(f"max_in{n}") for n in range(2)]
        trn_ps, exp_sb, sel_sb, av_ps = sem("trn_ps"), sem("exp_sb"), sem("sel_sb"), sem("av_ps")
        oT_sb, o_ps, rsum_sb, cn_sb = sem("oT_sb"), sem("o_ps"), sem("rsum_sb"), sem("cn_sb")
        cT_ps, cT_sb, proj_ps, h2_sb = sem("cT_ps"), sem("cT_sb"), sem("proj_ps"), sem("h2_sb")
        st2, mv2_sb, pool_var2, rstd2_sb, z3_sb = (sem(n) for n in ("st2", "mv2_sb", "pool_var2", "rstd2_sb", "z3_sb"))
        z3T_ps, z3T_sb, lg_ps, lg_sb, lgT_ps = (sem(n) for n in ("z3T_ps", "z3T_sb", "lg_ps", "lg_sb", "lgT_ps"))
        lmax_sb, ldiff_sb, lexp_sb, lsum_sb, gate_sb = (sem(n) for n in ("lmax_sb", "ldiff_sb", "lexp_sb", "lsum_sb", "gate_sb"))
        hit_sb, first_sb, onehot_sb = sem("hit_sb"), sem("first_sb"), sem("onehot_sb")
        rank_ps, pos_sb, slots_moved, own_sb, slotf_sb, slot_sb = (sem(n) for n in ("rank_ps", "pos_sb", "slots_moved", "own_sb", "slotf_sb", "slot_sb"))
        id_sb, token_moved = sem("id_sb"), sem("token_moved")
        scattered = [sem(f"scattered{n}") for n in range(4)]
        s_plan = sem("s_plan")
        passed_waits = sem("passed_waits")
        s_plan2 = sem("s_plan2")
        s_ptail = sem("s_ptail")
        pad_in = sem("pad_in")
        tail_in = sem("tail_in")
        t_in = [sem(f"t_in{n}") for n in range(RING)]
        tT_ps, tT_sb, hid_ps, hid_sb, hidT_ps, hidT_sb, y_ps, y_sb = (
            sem(n) for n in ("tT_ps", "tT_sb", "hid_ps", "hid_sb", "hidT_ps", "hidT_sb", "y_ps", "y_sb"))
        y_out = [sem(f"y_out{n}") for n in range(4)]

        class Row:

            def __init__(self, k, r, unroll=UNROLL):
                self.k, self.r, self.unroll = k, r, unroll
                self.n = unroll * k + r
                self.ap = bass.ds(self.n, 1)

            def lag(self, d):
                return Row(self.k, self.r - d, self.unroll)

            def live(self, rows=NB):
                return not isinstance(self.k, int) or 0 <= self.n < rows

        def wait_apart(eng):
            eng.sem_inc(passed_waits, 1)

        def wait(eng, s, b, per=1, upto=None, rows=NB):
            upto = per if upto is None else upto
            if isinstance(b.k, int):
                n, upto = (b.n, upto) if b.n < rows else (rows - 1, per)
                if per * n + upto > 0:
                    eng.wait_ge(s, per * n + upto)
            else:
                eng.wait_ge(s, b.k * (per * b.unroll) + (per * b.r + upto))
                if eng is nc.sync:
                    wait_apart(eng)

        def wait_dma(eng, ring, b, dmas=1, rows=NB):
            m = len(ring)
            if isinstance(b.k, int):
                if b.n >= 0:
                    eng.wait_ge(ring[b.n % m], 16 * dmas * (b.n // m + 1))
            else:
                eng.wait_ge(ring[b.r % m], b.k * (16 * dmas * b.unroll // m) + 16 * dmas * (b.r // m + 1))
                if eng is nc.sync:
                    wait_apart(eng)

        def bass_diag(a):
            return bass.AP(a.tensor, a.offset, [list(a.ap[0]), [T, 2], [1, HALF]])

        def pipeline(eng, step):
            start = LAST + 4
            loops = (NB - 2 - start) // UNROLL
            for i in range(start):
                step(Row(0, i))
            with eng.Fori(1, 1 + loops) as k:
                for j in range(UNROLL):
                    step(Row(k, start - UNROLL + j))
            for i in range(start + loops * UNROLL, NB + LAST):
                step(Row(0, i))

        def pipeline_b(eng, step, upto, lag=0):
            start = RING
            loops = (TILES - start) // RING
            for t in range(start):
                if t >= lag:
                    step(Row(0, t - lag, RING))
            with eng.Fori(0, loops) as k:
                for j in range(RING):
                    step(Row(k, start + j - lag, RING))
            for t in range(start + loops * RING, TILES + upto):
                step(Row(0, t - lag, RING))

        block = ctx.enter_context(nc.Block())

        @block.sync
        def _(sp):
            for dst, src in (
                (tok_w_sb[:], tok_w.rearrange("(k f) u -> f k u", k=TAPS)),
                (tok_b_sb[:], tok_b.rearrange("(a u) -> a u", a=1).partition_broadcast(128)),
                (w_qkv_sb[:], w_qkv),
                (gamma_sb[:], gamma.rearrange("(p a) -> p a", a=1)),
                (beta_sb[:], beta.rearrange("(p a) -> p a", a=1)),
                (w_out_sb[:], w_out),
                (b_out_sb[:], b_out.rearrange("(a u) -> a u", a=1)),
                (w_r_sb[:], w_r),
                (b_r_sb[:], b_r.rearrange("(p a) -> p a", a=1)),
            ):
                sp.dma_start(dst, src).then_inc(loads, 16)

            def load_x(b):
                wait(sp, xT_ps, b.lag(4))
                sp.dma_start(xt[:, b.r % 4, :, :], x[b.n].rearrange("(c p) f -> p c f", p=128)).then_inc(x_in[b.r % 4], 16)

            load_x(Row(0, 0))
            load_x(Row(0, 1))
            sp.wait_ge(s_const, 1)
            sp.dma_start(bins[E * BIN:E * BIN + 128, :], blank[:]).then_inc(pad_in, 16)

            def step(i):
                b = i.lag(-2)
                if b.live():
                    load_x(b)
                b = i.lag(1)
                if b.live():
                    d = b.r % 2
                    wait(sp, part3, b)
                    wait_dma(sp, stack_in, b.lag(2), dmas=9)
                    sp.dma_start(splits[d].rearrange("a s p t -> p (a s) t"),
                                 parts[:, d].rearrange("p a s t -> p (a s) t")).then_inc(split_out[d], 16)
                b = i.lag(3)
                if b.live():
                    wait(sp, nmT_sb, b)
                    wait(sp, trn_ps, b.lag(4), per=HEADS)
                    for s in range(PARTS):
                        sp.dma_start(Q[ROWS + s:ROWS + s + 1, b.r % 4], nmaxT[s * HEADS:(s + 1) * HEADS, b.r % 2, :]).then_inc(
                            max_in[b.r % 2], 16)
                b = i.lag(1)
                if b.live():
                    d, c = b.r % 2, b.r % 4
                    wait_dma(sp, split_out, b)
                    wait(sp, trn_ps, b.lag(4), per=HEADS)
                    rows = splits[d].rearrange("a s (d h) t -> a (s d) (h t)", h=HEADS)
                    for at, which in Q_SLOTS:
                        sp.dma_start(Q[at * HD:(at + len(which)) * HD, c].rearrange("p h t -> p (h t)"),
                                     rows[0, which[0] * HD:(which[-1] + 1) * HD, :]).then_inc(stack_in[d], 16)
                    for at, which in enumerate(K_SLOTS):
                        sp.dma_start(K[at * HD:(at + 1) * HD, c].rearrange("p h t -> p (h t)"),
                                     rows[1, which * HD:(which + 1) * HD, :]).then_inc(stack_in[d], 16)
                if isinstance(i.k, int) and i.n == 2:
                    for dst, src in (
                        (w_1_sb[:].rearrange("p (e f) -> p e f", e=E), w_1.rearrange("e h f -> h e f")),
                        (w_2_sb[:].rearrange("p (e f) -> p e f", e=E), w_2.rearrange("e h f -> h e f")),
                        (b_1_sb[:], b_1.rearrange("(a e) f -> a (e f)", a=1)),
                        (b_2_sb[:], b_2.rearrange("(a e) f -> a (e f)", a=1)),
                    ):
                        sp.dma_start(dst, src).then_inc(loads, 16)

            pipeline(sp, step)

            sp.wait_ge(s_plan, 1)
            for n in range(4):
                sp.wait_ge(scattered[n], 16 * 2 * NB // 4)
            for e in range(E):
                end = sp.value_load(tail_i[0:1, e:e + 1], min_val=e * BIN, max_val=e * BIN + TOKENS)
                sp.dma_start(bins[bass.ds(end, 128), :], blank[:]).then_inc(tail_in, 16)
            sp.wait_ge(tail_in, 16 * E)
            sp.wait_ge(pad_in, 16)

            def step_b(t):
                b = t.lag(RING)
                if not (isinstance(b.k, int) and b.n < 0):
                    wait_dma(sp, y_out, b, rows=TILES)
                row = sp.value_load(row_i[0:1, bass.ds(t.n, 1)], min_val=0, max_val=PAD_TILE)
                sp.dma_start(tile_in[:, t.r % RING, :], bins[bass.ds(row * 128, 128), :]).then_inc(t_in[t.r % RING], 16)

            pipeline_b(sp, step_b, upto=0)
            for n in range(4):
                sp.wait_ge(y_out[n], 16 * len(range(n, TILES, 4)))

        @block.gpsimd
        def _(pool):
            g = nc.gpsimd
            chain = [0]

            def link(ins):
                chain[0] += 1
                ins.then_inc(s_chain, 1)
                pool.wait_ge(s_chain, chain[0])

            link(g.memset(blank[:, 0:IDCOL], 0.0))
            link(g.memset(blank[:, IDCOL:REC].bitcast(I32), NO_TOKEN))
            link(g.memset(K[ROWS:MROWS], 1.0))
            link(g.memset(ident[:], 1.0))
            link(g.memset(causal[:], 0.0))
            link(g.memset(before[:], 1.0))
            link(g.memset(ones_bf[:], 1.0))
            link(g.memset(ones_row[:], 1.0))
            link(g.memset(neg_half[:], -0.5))
            link(g.memset(one_e[:], 1.0))
            link(g.memset(V[:], 0.0))
            link(g.memset(V[:, :, :, :, HD:HD + 1], 1.0))
            link(g.affine_select(out=ident[:], in_=ident[:], compare_op=ALU.is_equal, fill=0.0, base=0,
                                 pattern=[[-1, 128]], channel_multiplier=1))
            link(g.tensor_copy(ident_bf[:], ident[:]))
            link(g.affine_select(out=causal[:], in_=causal[:], compare_op=ALU.is_ge, fill=NEG, base=0,
                            pattern=[[0, 2], [-1, HALF]], channel_multiplier=1))
            link(g.affine_select(out=before[:], in_=before[:], compare_op=ALU.is_gt, fill=0.0, base=0,
                            pattern=[[1, HALF]], channel_multiplier=-1))
            link(g.iota(iota_i[:, 0:E], [[BIN, E]], base=0, channel_multiplier=0))
            link(g.iota(iota_i[:, E:2 * E], [[-1, E]], base=E, channel_multiplier=0))
            link(g.iota(token_i[:], [[HALF, 2]], base=0, channel_multiplier=1))
            link(g.iota(tile_no_i[:], [[1, TILES]], base=0, channel_multiplier=0))
            link(g.tensor_copy(bin_start[:], iota_i[:, 0:E]))
            link(g.tensor_copy(next_slot[:], iota_i[:, 0:E]))
            link(g.tensor_copy(rank_weight[:], iota_i[:, E:2 * E]))
            link(g.tensor_copy(token[:], token_i[:]))
            g.tensor_copy(tile_no[:], tile_no_i[:]).then_inc(s_const, 1)
            pool.wait_ge(s_const, 1)

            def keep_causal(b, hd):
                wait(pool, exp_sb, b, per=HEADS, upto=hd + 1)
                wait_apart(pool)
                v = P[0:HALF, hd, :]
                diag = bass_diag(v)
                g.affine_select(out=diag, in_=diag, compare_op=ALU.is_ge, fill=0.0, base=0,
                                pattern=[[0, 2], [1, HALF]], channel_multiplier=-1).then_inc(sel_sb, 1)

            def norm_factors(b):
                c = b.r % 2
                wait(pool, mv_sb, b)
                wait(pool, z_sb, b.lag(2), per=2)
                wait_apart(pool)
                g.tensor_scalar(var_e[0:HALF, 0:2], mv[0:HALF, c, :, 1], 1.0, EPS, ALU.mult, ALU.add)
                g.tensor_scalar(neg_m[0:HALF], mv[0:HALF, c, :, 0], -1.0, 0.0, ALU.mult, ALU.add)
                g.tensor_scalar(var_e[0:HALF, 2:4], mv[0:HALF, c, :, 1], 1.0 + EPS, EPS * EPS, ALU.mult,
                                ALU.add).then_inc(pool_var, 1)
                wait(pool, pool_var, b)
                g.tensor_tensor(rstd[0:HALF, c, :], var_e[0:HALF], neg_half[0:HALF], ALU.pow).then_inc(pool_rstd, 1)
                wait(pool, pool_rstd, b)
                g.tensor_tensor(neg_mr[0:HALF], neg_m[0:HALF], rstd[0:HALF, c, 0:2], ALU.mult)
                g.tensor_scalar(one_r[0:HALF], rstd[0:HALF, c, 0:2], 1.0, 1.0, ALU.mult, ALU.add).then_inc(pool_sc, 1)

            def residual(b):
                c = b.r % 2
                wait(pool, pool_sc, b)
                wait_apart(pool)
                for n in range(2):
                    g.tensor_scalar(base_h[0:HALF, n], h[0:HALF, c, n], one_r[0:HALF, n:n + 1],
                                    neg_mr[0:HALF, n:n + 1], ALU.mult, ALU.add).then_inc(base_part, 1)
                wait(pool, base_part, b, per=2)
                g.tensor_tensor(base[0:HALF, b.ap, :, :].rearrange("p a c u -> p (a c u)"),
                                base_h[0:HALF].rearrange("p c u -> p (c u)"),
                                o_bias[0:HALF].rearrange("p c u -> p (c u)"), ALU.add).then_inc(base_sb, 1)

            def norm_factor2(b):
                c = b.r % 2
                wait(pool, mv2_sb, b)
                wait(pool, z3_sb, b.lag(2), per=2)
                wait_apart(pool)
                g.tensor_scalar(var2_e[0:HALF], mv2[0:HALF, c, :, 1], 1.0, EPS, ALU.mult, ALU.add).then_inc(pool_var2, 1)
                wait(pool, pool_var2, b)
                g.tensor_tensor(rstd2[0:HALF, c, :], var2_e[0:HALF], neg_half[0:HALF, 0:2], ALU.pow).then_inc(rstd2_sb, 1)

            def scatter(b):
                c = b.r % 4
                wait(pool, slot_sb, b)
                wait(pool, gate_sb, b)
                wait(pool, id_sb, b)
                wait(pool, z3_sb, b, per=2)
                wait_apart(pool)
                for n in range(2):
                    g.indirect_dma_start(bins, bass.IndirectOffsetOnAxis(ap=slot[0:HALF, c, n:n + 1], axis=0),
                                         rec[0:HALF, c, n, :], None, bounds_check=E * BIN - 1,
                                         oob_is_err=False).then_inc(scattered[b.r % 4], 16)

            pool.wait_ge(s_setup, 1)

            def step(i):
                b, u, r = i.lag(4), i.lag(5), i.lag(6)
                for hd in range(HEADS):
                    if b.live():
                        keep_causal(b, hd)
                    if hd == 2 and i.live():
                        norm_factors(i)
                    if hd == 3 and i.live():
                        residual(i)
                    if hd == 6 and u.live():
                        norm_factor2(u)
                if r.live():
                    scatter(r)

            pipeline(pool, step)

            def step_b(t):
                c = t.r % 4
                wait(pool, y_sb, t, rows=TILES)
                wait_apart(pool)
                g.indirect_dma_start(out.rearrange("b t u -> (b t) u"),
                                     bass.IndirectOffsetOnAxis(ap=tile_in[:, t.r % RING, IDCOL:REC].bitcast(I32), axis=0),
                                     y[:, c, :], None, bounds_check=TOKENS - 1,
                                     oob_is_err=False).then_inc(y_out[c], 16)

            pipeline_b(pool, step_b, upto=3, lag=3)

        @block.scalar
        def _(act):
            a = nc.scalar

            def exp_scores(b, hd):
                wait(act, trn_ps, b, per=HEADS, upto=hd + 1)
                wait(act, av_ps, b.lag(1), per=HEADS, upto=hd + 1)
                a.activation(P[0:HALF, hd, :], ps[0:HALF, TRN + hd % 2, 0:TRI], ACT.Exp).then_inc(exp_sb, 1)

            def xT_copy(b):
                wait(act, xT_ps, b)
                wait(act, conv_ps, b.lag(2))
                a.copy(xT[:, b.r % 2, :], ps[:, M1, 0:TIN]).then_inc(xT_sb, 1)

            def zT_copy(b):
                wait(act, zT_ps, b)
                wait(act, v_ps, b.lag(2))
                a.copy(zT[:, b.r % 2, :], ps[:, M1, 0:T]).then_inc(zT_sb, 1)

            def qk_copy(b):
                c = b.r % 2
                wait(act, qk_ps, b)
                wait(act, rest1, b.lag(2))
                for n in range(2):
                    a.activation(qk[:, c, n, :], ps[:, M1, n * T:(n + 1) * T], ACT.Identity,
                                 bias=qk_bias[:, n:n + 1]).then_inc(qk_sb, 1)
                wait(act, qk_sb, b, per=2)
                wait_dma(act, split_out, b.lag(2))
                a.copy(parts[:, c, :, 0, :], qk[:, c]).then_inc(part1, 1)

            def second_parts(b):
                wait(act, rest1, b)
                a.copy(parts[:, b.r % 2, :, 1, :], rest[:, b.r % 2]).then_inc(part2, 1)

            def v_copy(b):
                wait(act, v_ps, b)
                wait(act, av_ps, b.lag(4), per=HEADS)
                a.copy(V[0:HALF, b.r % 4, :, :, 0:HD].rearrange("p c h d -> p (c h) d"),
                       ps[0:HALF, M0, 0:2 * D].rearrange("p (c d) -> p c d", d=HD)).then_inc(v_sb, 1)

            def nmaxT_copy(b):
                wait(act, nmT_ps, b)
                wait_dma(act, max_in, b.lag(2), dmas=PARTS)
                a.copy(nmaxT[:, b.r % 2, :], ps[0:PARTS * HEADS, MID, 0:T // 2 + 0].bitcast(BF16)[:, 0:T]).then_inc(nmT_sb, 1)

            def oT_copy(b):
                wait(act, av_ps, b, per=HEADS)
                wait(act, o_ps, b.lag(1))
                a.copy(oT[:], ps[:, AV, 0:2 * T].rearrange("p (c t) -> p c t", c=2)).then_inc(oT_sb, 1)

            def cT_copy(b):
                wait(act, cT_ps, b)
                wait(act, proj_ps, b.lag(2))
                a.copy(cT[:, b.r % 2, :], ps[:, M0, 0:T]).then_inc(cT_sb, 1)

            def z3T_copy(b):
                wait(act, z3T_ps, b)
                wait(act, lg_ps, b.lag(2))
                a.copy(z3T[:, b.r % 2, :], ps[:, M0, 0:T]).then_inc(z3T_sb, 1)

            def logit_copy(b):
                wait(act, lg_ps, b)
                wait(act, lgT_ps, b.lag(2))
                a.activation(logitT[:, b.r % 2, :], ps[0:E, M0, 0:T], ACT.Identity, bias=b_r_sb[:, 0:1]).then_inc(lg_sb, 1)

            def logit_exp(b):
                wait(act, ldiff_sb, b)
                wait(act, lsum_sb, b.lag(2))
                a.activation(lexp[0:HALF, b.r % 2], ldiff[0:HALF, b.r % 2], ACT.Exp).then_inc(lexp_sb, 1)

            act.wait_ge(s_setup, 1)
            act.wait_ge(s_const, 1)
            xT_copy(Row(0, 0))

            def step(i):
                s, b, u, r = i.lag(3), i.lag(4), i.lag(5), i.lag(6)
                for hd in range(HEADS):
                    if b.live():
                        exp_scores(b, hd)
                    if hd == 0:
                        if i.lag(1).live():
                            second_parts(i.lag(1))
                        if r.live():
                            z3T_copy(r)
                    if hd == 2:
                        if s.live():
                            nmaxT_copy(s)
                        if r.live():
                            logit_copy(r)
                        if u.live():
                            oT_copy(u)
                    if hd == 4:
                        if u.live():
                            cT_copy(u)
                        if r.live():
                            logit_exp(r)
                    if hd == 5 and i.live():
                        zT_copy(i)
                    if hd == 6 and i.live():
                        qk_copy(i)
                    if hd == 6 and i.lag(1).live():
                        v_copy(i.lag(1))
                    if hd == 7 and i.lag(-1).live():
                        xT_copy(i.lag(-1))

            pipeline(act, step)

            def step_b(t):
                if t.live(TILES):
                    wait(act, tT_ps, t, rows=TILES)
                    wait(act, hid_ps, t.lag(2), rows=TILES)
                    a.copy(tT[:, t.r % 2, :], ps[:, 0 + t.r % 2, 0:128]).then_inc(tT_sb, 1)
                b = t.lag(1)
                if b.live(TILES):
                    wait(act, hid_ps, b, rows=TILES)
                    wait(act, hidT_ps, b.lag(2), rows=TILES)
                    a.activation(hid[:, b.r % 2, :], ps[:, 2 + b.r % 2, 0:D], ACT.Relu).then_inc(hid_sb, 1)
                b = t.lag(2)
                if b.live(TILES):
                    wait(act, hidT_ps, b, rows=TILES)
                    wait(act, y_ps, b.lag(2), rows=TILES)
                    a.copy(hidT[:, b.r % 2, :], ps[:, 4 + b.r % 2, 0:128]).then_inc(hidT_sb, 1)

            pipeline_b(act, step_b, upto=2)

        @block.vector
        def _(dve):
            v = nc.vector
            dve.wait_ge(loads, 16 * 9)
            for n in range(2):
                v.tensor_copy(w_raw[:, n, :].rearrange("p (d h) -> p d h", h=HEADS),
                              w_qkv_sb[:, n * D:(n + 1) * D].rearrange("p (h d) -> p d h", h=HEADS)).then_inc(s_setup_pe, 1)
            scale = float(HD) ** -0.5
            v.tensor_scalar(gamma_q[:], gamma_sb[:], scale, None, ALU.mult).then_inc(s_setup_pe, 1)
            dve.wait_ge(s_setup_pe, 3)
            v.tensor_scalar(w_q[:], w_raw[:, 0, :], gamma_q[:, 0:1], None, ALU.mult)
            v.tensor_scalar(w_k[:], w_raw[:, 1, :], gamma_sb[:, 0:1], None, ALU.mult)
            v.tensor_scalar(w_v[:], w_qkv_sb[:, 2 * D:3 * D], gamma_sb[:, 0:1], None, ALU.mult)
            dve.wait_ge(s_ptail, 1)
            v.tensor_scalar(qk_bias[:, 0:1], ps[:, 4, 0:1], scale, None, ALU.mult)
            v.tensor_copy(qk_bias[:, 1:2], ps[:, 4, 1:2])
            v.tensor_copy(v_bias[:], ps[:, 4, 2:3]).then_inc(s_setup_pe, 1)
            dve.wait_ge(s_ptail, 2)
            v.tensor_tensor(o_bias_row[:], ps[0:1, 5, 0:D], b_out_sb[:], ALU.add).then_inc(s_setup_pe, 1)
            dve.wait_ge(s_ptail, 3)
            v.tensor_copy(o_bias[:, 0, :], ps[:, 4, 0:D])
            v.tensor_copy(o_bias[:, 1, :], ps[:, 4, 0:D]).then_inc(s_setup, 1)
            dve.wait_ge(s_const, 1)

            def row_max(b, hd):
                wait(dve, nat_ps, b, per=HEADS, upto=hd + 1)
                v.tensor_reduce(nmax3[0:HALF, b.r % 2, hd, :],
                                ps[0:HALF, NAT + hd % 2, 0:TRI].rearrange("p (c s) -> p c s", c=3),
                                AX.X, ALU.max, negate=True).then_inc(max_sb, 1)

            def max_parts(b):
                c = b.r % 2
                wait(dve, max_sb, b, per=HEADS)
                v.tensor_copy(nmax[0:HALF, 0, :], nmax3[0:HALF, c, :, 0])
                v.tensor_tensor(nmax[0:HALF, 1, :], nmax3[0:HALF, c, :, 1], nmax3[0:HALF, c, :, 2], ALU.min).then_inc(nm_sb, 1)
                wait(dve, nm_sb, b)
                wait(dve, nmT_ps, b.lag(2))
                v.tensor_copy(nmax_parts[0:HALF, c, :, 0, :], nmax[0:HALF]).then_inc(nmp1, 1)
                wait(dve, nmp1, b)
                v.tensor_tensor(nmax_rest[0:HALF], nmax[0:HALF], nmax_parts[0:HALF, c, :, 0, :], ALU.subtract).then_inc(nmr1, 1)
                wait(dve, nmr1, b)
                v.tensor_copy(nmax_parts[0:HALF, c, :, 1, :], nmax_rest[0:HALF]).then_inc(nmp2, 1)
                wait(dve, nmp2, b)
                v.tensor_tensor(nmax_parts[0:HALF, c, :, 2, :], nmax_rest[0:HALF], nmax_parts[0:HALF, c, :, 1, :],
                                ALU.subtract).then_inc(nmp3, 1)

            def third_parts(b):
                wait(dve, part2, b)
                v.tensor_tensor(parts[:, b.r % 2, :, 2, :], rest[:, b.r % 2], parts[:, b.r % 2, :, 1, :],
                                ALU.subtract).then_inc(part3, 1)

            def first_rest(b):
                c = b.r % 2
                wait(dve, part1, b)
                wait(dve, part3, b.lag(2))
                v.tensor_tensor(rest[:, c], qk[:, c], parts[:, c, :, 0, :], ALU.subtract).then_inc(rest1, 1)

            def tokens_and_stats(b):
                c = b.r % 2
                wait(dve, conv_ps, b)
                wait(dve, base_sb, b.lag(2))
                v.tensor_tensor(h[0:HALF, c], ps[0:HALF, M1, 0:2 * D].rearrange("p (c u) -> p c u", c=2),
                                tok_b_sb[0:HALF, None, :].to_broadcast([HALF, 2, D]), ALU.add).then_inc(h_sb, 1)
                wait(dve, h_sb, b)
                for n in range(2):
                    v.bn_stats(stats[0:HALF, n, :], h[0:HALF, c, n, :]).then_inc(st1, 1)
                wait(dve, st1, b, per=2)
                wait_apart(dve)
                v.bn_aggr(mv[0:HALF, c, 0, :], stats[0:HALF, 0, :])
                v.bn_aggr(mv[0:HALF, c, 1, :], stats[0:HALF, 1, :]).then_inc(mv_sb, 1)

            def normalise(b):
                c = b.r % 2
                wait(dve, pool_rstd, b)
                wait(dve, zT_ps, b.lag(2))
                for n in range(2):
                    v.tensor_scalar(z[0:HALF, c, n], h[0:HALF, c, n], mv[0:HALF, c, n, 0:1],
                                    rstd[0:HALF, c, 2 + n:3 + n], ALU.subtract, ALU.mult).then_inc(z_sb, 1)

            def divide(b):
                wait(dve, o_ps, b)
                o = ps[0:HALF, MID, :].rearrange("p (g c) -> p g c", c=32)
                v.reciprocal(rsum[0:HALF], o[:, :, HD]).then_inc(rsum_sb, 1)
                wait(dve, rsum_sb, b)
                wait(dve, cT_ps, b.lag(2))
                v.tensor_tensor(cn[0:HALF, b.r % 2].rearrange("p c (h d) -> p (c h) d", d=HD), o[:, :, 0:HD],
                                rsum[0:HALF, :, None].to_broadcast([HALF, 16, HD]), ALU.mult).then_inc(cn_sb, 1)

            def residual_and_stats(b):
                c = b.r % 2
                wait(dve, proj_ps, b)
                wait(dve, base_sb, b)
                wait_dma(dve, scattered, b.lag(4), dmas=2)
                v.tensor_tensor(rec[0:HALF, b.r % 4, :, D:2 * D], ps[0:HALF, M0, 0:2 * D].rearrange("p (c u) -> p c u", c=2),
                                base[0:HALF, b.ap, :, :].rearrange("p a c u -> p (a c) u"), ALU.add).then_inc(h2_sb, 1)
                wait(dve, h2_sb, b)
                for n in range(2):
                    v.bn_stats(stats2[0:HALF, n, :], rec[0:HALF, b.r % 4, n, D:2 * D]).then_inc(st2, 1)
                wait(dve, st2, b, per=2)
                wait_apart(dve)
                v.bn_aggr(mv2[0:HALF, c, 0, :], stats2[0:HALF, 0, :])
                v.bn_aggr(mv2[0:HALF, c, 1, :], stats2[0:HALF, 1, :]).then_inc(mv2_sb, 1)

            def normalise2(b):
                c = b.r % 2
                wait(dve, rstd2_sb, b)
                for n in range(2):
                    v.tensor_scalar(rec[0:HALF, b.r % 4, n, 0:D], rec[0:HALF, b.r % 4, n, D:2 * D], mv2[0:HALF, c, n, 0:1],
                                    rstd2[0:HALF, c, n:n + 1], ALU.subtract, ALU.mult).then_inc(z3_sb, 1)

            def route(b):
                c = b.r % 2
                wait(dve, lgT_ps, b)
                lg = ps[0:HALF, M1, 0:2 * E].rearrange("p (c e) -> p c e", e=E)
                v.tensor_reduce(lmax[0:HALF], lg, AX.X, ALU.max).then_inc(lmax_sb, 1)
                wait(dve, lmax_sb, b)
                wait(dve, lexp_sb, b.lag(2))
                v.tensor_tensor(ldiff[0:HALF, c], lg, lmax[0:HALF, :, None].to_broadcast([HALF, 2, E]),
                                ALU.subtract).then_inc(ldiff_sb, 1)
                wait(dve, ldiff_sb, b)
                v.scalar_tensor_tensor(hit[0:HALF], ldiff[0:HALF, c], 0.0,
                                       rank_weight[0:HALF, None, :].to_broadcast([HALF, 2, E]),
                                       ALU.is_equal, ALU.mult).then_inc(hit_sb, 1)
                wait(dve, hit_sb, b)
                v.tensor_reduce(first[0:HALF], hit[0:HALF], AX.X, ALU.max).then_inc(first_sb, 1)
                wait(dve, first_sb, b)
                wait(dve, rank_ps, b.lag(2))
                v.tensor_tensor(onehot[0:HALF, c], hit[0:HALF], first[0:HALF, :, None].to_broadcast([HALF, 2, E]),
                                ALU.is_equal).then_inc(onehot_sb, 1)

            def gate_and_id(b):
                wait(dve, lexp_sb, b)
                wait_dma(dve, scattered, b.lag(4), dmas=2)
                v.tensor_copy(rec[0:HALF, b.r % 4, :, IDCOL].bitcast(I32), token[0:HALF]).then_inc(id_sb, 1)
                v.tensor_reduce(lsum[0:HALF], lexp[0:HALF, b.r % 2], AX.X, ALU.add).then_inc(lsum_sb, 1)
                wait(dve, lsum_sb, b)
                v.reciprocal(rec[0:HALF, b.r % 4, :, GATE], lsum[0:HALF]).then_inc(gate_sb, 1)
                v.tensor_scalar(token[0:HALF], token[0:HALF], float(T), None, ALU.add).then_inc(token_moved, 1)

            def slots(b):
                c = b.r % 2
                wait(dve, rank_ps, b)
                wait(dve, slots_moved, b.lag(1))
                v.tensor_tensor(pos[0:HALF], ps[0:HALF, MID, 0:2 * E].rearrange("p (c e) -> p c e", e=E),
                                next_slot[0:HALF, None, :].to_broadcast([HALF, 2, E]), ALU.add).then_inc(pos_sb, 1)
                wait(dve, pos_sb, b)
                v.tensor_tensor(next_slot[0:HALF], ps[0:HALF, MID, 2 * E:3 * E], next_slot[0:HALF], ALU.add).then_inc(slots_moved, 1)
                v.tensor_tensor(pos_own[0:HALF], pos[0:HALF], onehot[0:HALF, c], ALU.mult).then_inc(own_sb, 1)
                wait(dve, own_sb, b)
                v.tensor_reduce(slot_f[0:HALF], pos_own[0:HALF], AX.X, ALU.add).then_inc(slotf_sb, 1)
                wait(dve, slotf_sb, b)
                v.tensor_copy(slot[0:HALF, b.r % 4, :], slot_f[0:HALF]).then_inc(slot_sb, 1)

            def step(i):
                n, s, u, r = i.lag(2), i.lag(3), i.lag(5), i.lag(6)
                for hd in range(HEADS):
                    if hd == 0 and s.live():
                        max_parts(s)
                    if n.live():
                        row_max(n, hd)
                    if hd == 1 and i.lag(1).live():
                        third_parts(i.lag(1))
                    if hd == 2 and i.live():
                        tokens_and_stats(i)
                    if hd == 3:
                        if u.live():
                            divide(u)
                        if r.live():
                            route(r)
                    if hd == 4:
                        if i.live():
                            normalise(i)
                    if hd == 5 and r.live():
                        gate_and_id(r)
                    if hd == 6 and u.live():
                        residual_and_stats(u)
                    if hd == 7:
                        if r.live():
                            slots(r)
                        if i.live():
                            first_rest(i)
                        if u.live():
                            normalise2(u)

            pipeline(dve, step)

            chain = [0]

            def link(ins):
                chain[0] += 1
                ins.then_inc(s_plan2, 1)
                dve.wait_ge(s_plan2, chain[0])

            dve.wait_ge(slots_moved, NB)
            v.tensor_copy(tail_i[:], next_slot[0:1])
            link(v.tensor_tensor(count[:], next_slot[0:1], bin_start[0:1], ALU.subtract))
            link(v.tensor_scalar(count[:], count[:], 127.0, None, ALU.add))
            link(v.tensor_copy(count_i[:], count[:]))
            link(v.tensor_scalar(tiles_i[:], count_i[:], 7, None, ALU.logical_shift_right))
            link(v.tensor_copy(tiles_f[:], tiles_i[:]))
            link(v.tensor_tensor_scan(tiles_end[:], one_e[:], tiles_f[:], 0.0, ALU.mult, ALU.add))
            link(v.tensor_tensor(passed[:], tiles_end[:, None, :].to_broadcast([1, TILES, E]),
                                 tile_no[:, :, None].to_broadcast([1, TILES, E]), ALU.is_le))
            link(v.tensor_reduce(expert_f[:], passed[:], AX.X, ALU.add))
            link(v.tensor_tensor(skipped[:], passed[:], tiles_f[:, None, :].to_broadcast([1, TILES, E]), ALU.mult))
            link(v.tensor_reduce(start_f[:], skipped[:], AX.X, ALU.add))
            link(v.tensor_tensor(row_f[:], tile_no[:], start_f[:], ALU.subtract))
            link(v.tensor_scalar(row_a[:], expert_f[:], float(BIN // 128), None, ALU.mult))
            link(v.tensor_tensor(row_b[:], row_a[:], row_f[:], ALU.add))
            link(v.tensor_scalar(row_a[:], row_b[:], float(PAD_TILE), None, ALU.min))
            link(v.tensor_scalar(expert_c[:], expert_f[:], float(E - 1), float(D), ALU.min, ALU.mult))
            link(v.tensor_copy(row_i[:], row_a[:]))
            v.tensor_copy(expert_i[:], expert_c[:]).then_inc(s_plan, 1)

            def step_b(t):
                wait(dve, y_ps, t, rows=TILES)
                b = t.lag(4)
                if not (isinstance(b.k, int) and b.n < 0):
                    wait_dma(dve, y_out, b, rows=TILES)
                v.scalar_tensor_tensor(y[:, t.r % 4, :], ps[:, 6 + t.r % 2, 0:D], tile_in[:, t.r % RING, GATE:GATE + 1],
                                       tile_in[:, t.r % RING, D:2 * D], ALU.mult, ALU.add).then_inc(y_sb, 1)

            pipeline_b(dve, step_b, upto=3, lag=3)

        @block.tensor
        def _(pe):
            mm, tp = nc.tensor.matmul, nc.tensor.transpose
            pe.wait_ge(loads, 16 * 9)
            pe.wait_ge(s_setup_pe, 3)
            pe.wait_ge(s_const, 1)
            mm(ps[:, 4, 0:1], w_raw[:, 0, :], beta_sb[:], start=True, stop=True)
            mm(ps[:, 4, 1:2], w_raw[:, 1, :], beta_sb[:], start=True, stop=True)
            mm(ps[:, 4, 2:3], w_qkv_sb[:, 2 * D:3 * D], beta_sb[:], start=True, stop=True).then_inc(s_ptail, 1)
            pe.wait_ge(s_setup_pe, 4)
            mm(ps[0:1, 5, 0:D], v_bias[:], w_out_sb[:], start=True, stop=True).then_inc(s_ptail, 1)
            pe.wait_ge(s_setup_pe, 5)
            mm(ps[:, 4, 0:D], ones_row[:], o_bias_row[:], start=True, stop=True).then_inc(s_ptail, 1)
            pe.wait_ge(s_setup, 1)

            def x_transpose(b):
                wait_dma(pe, x_in, b)
                wait(pe, qk_sb, b.lag(1), per=2)
                for n in range(2):
                    last = tp(ps[:, M1, n * 128:(n + 1) * 128], xt[:, b.r % 4, n, :], ident[:])
                last.then_inc(xT_ps, 1)

            def conv(b, n):
                if n == 0:
                    wait(pe, xT_sb, b)
                for k in range(TAPS):
                    last = mm(ps[0:HALF, M1, n * D:(n + 1) * D], xT[:, b.r % 2, n * HALF + k:(n + 1) * HALF + k],
                              tok_w_sb[:, k, :], start=(k == 0), stop=(k == TAPS - 1))
                if n == 1:
                    last.then_inc(conv_ps, 1)

            def z_transpose(b):
                wait(pe, z_sb, b, per=2)
                wait(pe, ldiff_sb, b.lag(6))
                for n in range(2):
                    last = tp(ps[:, M1, n * HALF:(n + 1) * HALF], z[0:HALF, b.r % 2, n, :], ident[0:HALF, 0:HALF])
                last.then_inc(zT_ps, 1)

            def project_qk(b):
                wait(pe, zT_sb, b)
                for n, w in enumerate((w_q, w_k)):
                    last = mm(ps[:, M1, n * T:(n + 1) * T], w[:], zT[:, b.r % 2, :], start=True, stop=True)
                last.then_inc(qk_ps, 1)

            def project_v(b):
                wait(pe, h2_sb, b.lag(4))
                wait(pe, v_sb, b.lag(1))
                for n in range(2):
                    last = mm(ps[0:HALF, M0, n * D:(n + 1) * D], zT[:, b.r % 2, n * HALF:(n + 1) * HALF], w_v[:],
                              start=True, stop=True)
                last.then_inc(v_ps, 1)

            def scores(b, hd):
                if hd == 0:
                    wait_dma(pe, stack_in, b, dmas=9)
                c, bank = b.r % 4, NAT + hd % 2
                wait(pe, max_sb, b, per=HEADS, upto=hd - 1)
                mm(ps[0:HALF, bank, 0:HALF], Q[0:ROWS, c, hd, 0:HALF], K[0:ROWS, c, hd, 0:HALF], start=True, stop=False,
                   skip_group_check=True)
                mm(ps[0:HALF, bank, HALF:TRI], Q[0:ROWS, c, hd, HALF:T], K[0:ROWS, c, hd, :], start=False, stop=False,
                   skip_group_check=True)
                mm(bass_diag(ps[0:HALF, bank, 0:TRI]), ident_bf[0:HALF, 0:HALF], causal[0:HALF], start=False, stop=True,
                   skip_group_check=True).then_inc(nat_ps, 1)

            def scores_T(b, hd):
                if hd == 0:
                    wait_dma(pe, max_in, b, dmas=PARTS)
                c, bank = b.r % 4, TRN + hd % 2
                wait(pe, exp_sb, b, per=HEADS, upto=hd - 1)
                mm(ps[0:HALF, bank, 0:T], K[0:MROWS, c, hd, 0:HALF], Q[0:MROWS, c, hd, :], start=True, stop=True,
                   skip_group_check=True)
                mm(ps[0:HALF, bank, T:TRI], K[0:MROWS, c, hd, HALF:T], Q[0:MROWS, c, hd, HALF:T], start=False, stop=True,
                   skip_group_check=True).then_inc(trn_ps, 1)

            def values(b, hd):
                if hd == 0:
                    wait(pe, oT_sb, b.lag(1))
                    wait(pe, v_sb, b)
                wait(pe, sel_sb, b, per=HEADS, upto=hd + 1)
                c, s, j = b.r % 4, hd // 4, 32 * (hd % 4)
                mm(ps[j:j + 32, AV, s * T:(s + 1) * T], V[0:HALF, c, 0, hd, :], P[0:HALF, hd, 0:T], start=True, stop=False,
                   skip_group_check=True)
                mm(ps[j:j + 32, AV, s * T + HALF:(s + 1) * T], V[0:HALF, c, 1, hd, :], P[0:HALF, hd, T:TRI],
                   start=False, stop=True, skip_group_check=True).then_inc(av_ps, 1)

            def max_transpose(b):
                wait(pe, nmp3, b)
                wait(pe, slots_moved, b.lag(4))
                wait(pe, cn_sb, b.lag(3))
                wait(pe, nmT_sb, b.lag(1))
                for n in range(2):
                    last = tp(ps[0:PARTS * HEADS, MID, n * HALF // 2:(n + 1) * HALF // 2].bitcast(BF16),
                              nmax_parts[0:HALF, b.r % 2, n].rearrange("p s h -> p (s h)"), ident_bf[0:HALF, 0:HALF])
                last.then_inc(nmT_ps, 1)

            def heads_transpose(b):
                wait(pe, oT_sb, b)
                wait(pe, nmT_sb, b.lag(-2))
                wait(pe, slots_moved, b.lag(2))
                for n in range(2):
                    for s in range(2):
                        last = tp(ps[0:HALF, MID, (2 * n + s) * 128:(2 * n + s + 1) * 128],
                                  oT[:, s, n * HALF:(n + 1) * HALF], ident[:])
                last.then_inc(o_ps, 1)

            def c_transpose(b):
                wait(pe, cn_sb, b)
                wait(pe, lg_sb, b.lag(1))
                wait(pe, v_sb, b.lag(-3))
                for n in range(2):
                    last = tp(ps[:, M0, n * HALF:(n + 1) * HALF], cn[0:HALF, b.r % 2, n, :], ident[0:HALF, 0:HALF])
                last.then_inc(cT_ps, 1)

            def project_out(b):
                wait(pe, cT_sb, b)
                for n in range(2):
                    last = mm(ps[0:HALF, M0, n * D:(n + 1) * D], cT[:, b.r % 2, n * HALF:(n + 1) * HALF], w_out_sb[:],
                              start=True, stop=True)
                last.then_inc(proj_ps, 1)

            def z3_transpose(b):
                wait(pe, z3_sb, b, per=2)
                wait(pe, v_sb, b.lag(-4))
                for n in range(2):
                    last = tp(ps[:, M0, n * HALF:(n + 1) * HALF], rec[0:HALF, b.r % 4, n, 0:D], ident[0:HALF, 0:HALF])
                last.then_inc(z3T_ps, 1)

            def logits(b):
                wait(pe, z3T_sb, b)
                mm(ps[0:E, M0, 0:T], w_r_sb[:], z3T[:, b.r % 2, :], start=True, stop=True).then_inc(lg_ps, 1)

            def logits_transpose(b):
                wait(pe, lg_sb, b)
                wait(pe, h_sb, b.lag(-6))
                wait(pe, ldiff_sb, b.lag(1))
                wait_apart(pe)
                for n in range(2):
                    last = tp(ps[0:HALF, M1, n * E:(n + 1) * E], logitT[:, b.r % 2, n * HALF:(n + 1) * HALF],
                              ident[0:E, 0:E])
                last.then_inc(lgT_ps, 1)

            def ranks(b):
                wait(pe, onehot_sb, b)
                wait(pe, cn_sb, b.lag(-1))
                wait(pe, slots_moved, b.lag(1))
                oh = onehot[0:HALF, b.r % 2]
                mm(ps[0:HALF, MID, 0:2 * E], before[0:HALF], oh.rearrange("p c e -> p (c e)"), start=True, stop=False,
                   skip_group_check=True)
                mm(ps[0:HALF, MID, E:2 * E], ones_bf[0:HALF], oh[:, 0, :], start=False, stop=True, skip_group_check=True)
                for n in range(2):
                    last = mm(ps[0:HALF, MID, 2 * E:3 * E], ones_bf[0:HALF], oh[:, n, :], start=False, stop=(n == 1),
                              skip_group_check=True)
                last.then_inc(rank_ps, 1)

            x_transpose(Row(0, 0))

            def step(i):
                n, s, b, u, r = i.lag(2), i.lag(3), i.lag(4), i.lag(5), i.lag(6)
                for hd in range(HEADS):
                    if b.live():
                        scores_T(b, hd)
                    if n.live():
                        scores(n, hd)
                    if hd == 0:
                        if r.live():
                            z3_transpose(r)
                        if i.live():
                            conv(i, 0)
                    if hd == 1:
                        if s.live():
                            max_transpose(s)
                        if i.live():
                            conv(i, 1)
                    if hd == 2 and r.live():
                        logits(r)
                    if hd == 3:
                        if u.live():
                            heads_transpose(u)
                        if r.live():
                            logits_transpose(r)
                    if hd == 4 and u.live():
                        c_transpose(u)
                    if hd == 5:
                        if i.live():
                            z_transpose(i)
                        if u.live():
                            project_out(u)
                    if hd == 6:
                        if i.live():
                            project_qk(i)
                        if i.lag(1).live():
                            project_v(i.lag(1))
                        if r.live():
                            ranks(r)
                    if hd == 7 and i.lag(-1).live():
                        x_transpose(i.lag(-1))
                    if hd < 2:
                        if u.live():
                            values(u, hd + 6)
                    elif b.live():
                        values(b, hd - 2)

            pipeline(pe, step)
            pe.wait_ge(s_plan, 1)
            pe.wait_ge(loads, 16 * 13)

            def step_b(t):
                if t.live(TILES):
                    wait_dma(pe, t_in, t, rows=TILES)
                    wait(pe, tT_sb, t.lag(2), rows=TILES)
                    tp(ps[:, 0 + t.r % 2, 0:128], tile_in[:, t.r % RING, 0:D], ident[:]).then_inc(tT_ps, 1)
                b = t.lag(1)
                if b.live(TILES):
                    c = b.r % 2
                    e = pe.value_load(expert_i[0:1, bass.ds(b.n, 1)], min_val=0, max_val=(E - 1) * D)
                    wait(pe, tT_sb, b, rows=TILES)
                    wait(pe, hid_sb, b.lag(2), rows=TILES)
                    mm(ps[:, 2 + c, 0:D], tT[:, c, :], w_1_sb[:, bass.ds(e, D)], start=True, stop=False)
                    mm(ps[:, 2 + c, 0:D], ones_row[:], b_1_sb[:, bass.ds(e, D)], start=False, stop=True).then_inc(hid_ps, 1)
                b = t.lag(2)
                if b.live(TILES):
                    c = b.r % 2
                    wait(pe, hid_sb, b, rows=TILES)
                    wait(pe, hidT_sb, b.lag(2), rows=TILES)
                    tp(ps[:, 4 + c, 0:128], hid[:, c, :], ident[:]).then_inc(hidT_ps, 1)
                b = t.lag(3)
                if b.live(TILES):
                    c = b.r % 2
                    e = pe.value_load(expert_i[0:1, bass.ds(b.n, 1)], min_val=0, max_val=(E - 1) * D)
                    wait(pe, hidT_sb, b, rows=TILES)
                    wait(pe, y_sb, b.lag(2), rows=TILES)
                    mm(ps[:, 6 + c, 0:D], hidT[:, c, :], w_2_sb[:, bass.ds(e, D)], start=True, stop=False)
                    mm(ps[:, 6 + c, 0:D], ones_row[:], b_2_sb[:, bass.ds(e, D)], start=False, stop=True).then_inc(y_ps, 1)

            pipeline_b(pe, step_b, upto=3)


_INS = ["x", "L0_tok_W", "L0_tok_b", "L0_attn_w_qkv", "L0_attn_w_out", "L0_attn_b_out", "L0_attn_gamma", "L0_attn_beta",
        "L0_ffn_Wr", "L0_ffn_br", "L0_ffn_W1", "L0_ffn_b1", "L0_ffn_W2", "L0_ffn_b2"]


def kernel(**inputs):
    import numpy as _np
    import concourse.bacc as _bacc
    from concourse import mybir as _mybir
    from concourse.bass_utils import run_bass_kernel_spmd as _run

    nc = _bacc.Bacc("TRN2", target_bir_lowering=False, num_devices=1)
    arrays, args = {}, []
    for name in _INS:
        a = _np.ascontiguousarray(inputs[name])
        arrays[f"in_{name}_dram"] = a
        args.append(nc.dram_tensor(f"in_{name}_dram", a.shape, _mybir.dt.from_np(a.dtype), kind="ExternalInput").ap())
    b, t, d = inputs["x"].shape
    taps = inputs["L0_tok_W"].shape[0] // d
    shape = (b, t - taps + 1, d)
    args.append(nc.dram_tensor("out_0_dram", shape, _mybir.dt.float32, kind="ExternalOutput").ap())
    build(nc, *args)
    r = _run(nc, [arrays], core_ids=[0])
    return r.results[0]["out_0_dram"]
```

```python
from contextlib import ExitStack

import concourse.bass as bass
from concourse import mybir

F32 = mybir.dt.float32
BF16 = mybir.dt.bfloat16
I32 = mybir.dt.int32
ALU = mybir.AluOpType
ACT = mybir.ActivationFunctionType
AX = mybir.AxisListType

EPS = 1e-5
HEADS = 8
NEG = -1e30
UNROLL = 4


def build(nc, x, tok_w, tok_b, w_qkv, w_out, b_out, gamma, beta, w_r, b_r, w_1, b_1, w_2, b_2, out):
    NB, TIN, D = x.shape
    TAPS = tok_w.shape[0] // D
    T = TIN - TAPS + 1
    HALF = T // 2
    HD = D // HEADS
    E = w_r.shape[1]
    TOKENS = NB * T
    TRI = 3 * HALF
    REC = 2 * D + 2
    GATE, IDCOL = 2 * D, 2 * D + 1
    BIN = 64 * 128
    TILES = TOKENS // 128 + E - 1
    PAD_TILE = E * BIN // 128
    NO_TOKEN = 1 << 20
    PARTS = 3
    ROWS = 6 * HD
    STACKS = [(0, 0, 1, ((0, 2), (1, 2 * HD))), (1, 0, 3, ((0, 2), (1, HD))), (1, 2 * HD, 4, ((0, 2), (1, HD))),
              (0, 4 * HD, 0, ((2 * HD, 2), (1, HD))), (1, 4 * HD, 3, ((2 * HD, 2), (1, HD)))]
    MROWS = ROWS + PARTS
    LAST = 7
    assert TOKENS % 128 == 0 and T % 2 == 0 and TOKENS + 128 <= BIN and D == 128 and E == 8

    bins = nc.dram_tensor("bins", [E * BIN + 128, REC], F32, kind="Internal").ap()
    splits = nc.dram_tensor("splits", [2, 2 * PARTS, 128, T], BF16, kind="Internal").ap()

    with ExitStack() as ctx:
        def sb(name, shape, dt=F32):
            return ctx.enter_context(nc.sbuf_tensor(name, shape, dt))

        def sem(name):
            return ctx.enter_context(nc.semaphore(name))

        tok_w_sb = sb("tok_w_sb", [128, TAPS, D])
        w_qkv_sb = sb("w_qkv_sb", [128, 3 * D])
        w_out_sb = sb("w_out_sb", [128, D])
        gamma_sb = sb("gamma_sb", [128, 1])
        beta_sb = sb("beta_sb", [128, 1])
        tok_b_sb = sb("tok_b_sb", [128, D])
        b_out_sb = sb("b_out_sb", [1, D])
        w_r_sb = sb("w_r_sb", [128, D])
        b_r_sb = sb("b_r_sb", [128, E])
        lg = sb("lg", [128, 2, E])
        W_COLS = 2 * D + 1
        experts = sb("experts", [128, E, W_COLS])
        b_2_sb = sb("b_2_sb", [128, E, D])
        w_raw = sb("w_raw", [128, 2, D])
        w_q = sb("w_q", [128, D])
        w_k = sb("w_k", [128, D])
        w_v = sb("w_v", [128, D])
        gamma_q = sb("gamma_q", [128, 1])
        qk_bias = sb("qk_bias", [128, 2])
        v_bias = sb("v_bias", [128, 1])
        o_bias_row = sb("o_bias_row", [1, D])
        o_bias = sb("o_bias", [128, 2, D])
        ident = sb("ident", [128, 128])
        ident_bf = sb("ident_bf", [128, 128], BF16)
        causal = sb("causal", [128, 2, HALF], BF16)
        before = sb("before", [128, HALF], BF16)
        ones_bf = sb("ones_bf", [128, HALF], BF16)
        ones_row = sb("ones_row", [1, 128])
        neg_half = sb("neg_half", [128, 4])
        iota_i = sb("iota_i", [128, 2 * E], I32)
        bin_start = sb("bin_start", [128, E])
        rank_weight = sb("rank_weight", [128, E])
        token_i = sb("token_i", [128, 2], I32)
        token = sb("token", [128, 2])
        next_slot = sb("next_slot", [128, E])
        blank = sb("blank", [128, REC])

        xt = sb("xt", [128, 4, 2, D])
        xT = sb("xT", [128, 2, TIN])
        h = sb("h", [128, 2, 2, D])
        stats = sb("stats", [128, 2, 6])
        mv = sb("mv", [128, 2, 2, 2])
        var_e = sb("var_e", [128, 4])
        rstd = sb("rstd", [128, 2, 4])
        one_r = sb("one_r", [128, 2])
        neg_m = sb("neg_m", [128, 2])
        neg_mr = sb("neg_mr", [128, 2])
        base_h = sb("base_h", [128, 2, D])
        base = sb("base", [128, NB, 2, D])
        z = sb("z", [128, 2, 2, D])
        zT = sb("zT", [128, 2, T])
        qk = sb("qk", [128, 2, 2, T])
        rest = sb("rest", [128, 2, 2, T])
        parts = sb("parts", [128, 2, 2 * PARTS, T], BF16)
        Q = sb("Q", [128, 4, HEADS, T], BF16)
        K = sb("K", [128, 4, HEADS, T], BF16)
        V = sb("V", [128, 4, 2, HEADS, 32])
        nmax3 = sb("nmax3", [128, 2, HEADS, 3])
        nmax = sb("nmax", [128, 2, HEADS])
        nmax_rest = sb("nmax_rest", [128, 2, HEADS])
        nmax_parts = sb("nmax_parts", [128, 2, 2, PARTS, HEADS], BF16)
        nmaxT = sb("nmaxT", [PARTS * HEADS, 2, T], BF16)
        P = sb("P", [128, HEADS, TRI])
        oT = sb("oT", [128, 2, T])
        rsum = sb("rsum", [128, 16])
        cn = sb("cn", [128, 2, 2, D])
        cT = sb("cT", [128, 2, T])
        rec = sb("rec", [128, 4, 2, REC])
        stats2 = sb("stats2", [128, 2, 6])
        mv2 = sb("mv2", [128, 2, 2, 2])
        var2_e = sb("var2_e", [128, 2])
        rstd2 = sb("rstd2", [128, 2, 2])
        z3T = sb("z3T", [128, 2, T])
        lmax = sb("lmax", [128, 2])
        ldiff = sb("ldiff", [128, 2, 2, E])
        lexp = sb("lexp", [128, 2, 2, E])
        lsum = sb("lsum", [128, 2])
        hit = sb("hit", [128, 2, E])
        first = sb("first", [128, 2])
        onehot = sb("onehot", [128, 2, 2, E], BF16)
        pos = sb("pos", [128, 2, E])
        pos_own = sb("pos_own", [128, 2, E])
        slot_f = sb("slot_f", [128, 2])
        slot = sb("slot", [128, 4, 2], I32)

        RING = 8
        tile_in = sb("tile_in", [128, RING, REC])
        tT = sb("tT", [128, 2, 128])
        b_1_rows = sb("b_1_rows", [E, D])
        expert = sb("expert", [128, 4, W_COLS])
        hidT = sb("hidT", [128, 2, 128])
        y_part = sb("y_part", [128, 2, D])
        y = sb("y", [128, 4, D])
        count = sb("count", [1, E])
        count_i = sb("count_i", [1, E], I32)
        tiles_i = sb("tiles_i", [1, E], I32)
        tiles_f = sb("tiles_f", [1, E])
        tiles_end = sb("tiles_end", [1, E])
        one_e = sb("one_e", [1, E])
        tile_no_i = sb("tile_no_i", [1, TILES], I32)
        tile_no = sb("tile_no", [1, TILES])
        passed = sb("passed", [1, TILES, E])
        skipped = sb("skipped", [1, TILES, E])
        expert_f = sb("expert_f", [1, TILES])
        start_f = sb("start_f", [1, TILES])
        row_f = sb("row_f", [1, TILES])
        row_a = sb("row_a", [1, TILES])
        row_b = sb("row_b", [1, TILES])
        expert_c = sb("expert_c", [1, TILES])
        row_i = sb("row_i", [1, TILES], I32)
        expert_i = sb("expert_i", [1, TILES], I32)
        tail_i = sb("tail_i", [1, E], I32)

        ps = ctx.enter_context(nc.psum_tensor("ps", [128, 8, 512], F32))
        NAT, TRN, AV, MID, M0, M1 = 0, 2, 4, 5, 6, 7

        loads = sem("loads")
        s_const = sem("s_const")
        s_chain = sem("s_chain")
        s_setup_pe = sem("s_setup_pe")
        s_setup = sem("s_setup")
        x_in = [sem(f"x_in{n}") for n in range(4)]
        xT_ps, xT_sb = sem("xT_ps"), sem("xT_sb")
        conv_ps, h_sb, st1, mv_sb = sem("conv_ps"), sem("h_sb"), sem("st1"), sem("mv_sb")
        pool_var, pool_rstd, pool_sc, base_part, base_sb = (sem(n) for n in ("pool_var", "pool_rstd", "pool_sc", "base_part", "base_sb"))
        z_sb, zT_ps, zT_sb = sem("z_sb"), sem("zT_ps"), sem("zT_sb")
        qk_ps, qk_sb, v_ps, v_sb = sem("qk_ps"), sem("qk_sb"), sem("v_ps"), sem("v_sb")
        part1, rest1, part2, part3 = sem("part1"), sem("rest1"), sem("part2"), sem("part3")
        split_out = [sem(f"split_out{n}") for n in range(2)]
        stack_in = [sem(f"stack_in{n}") for n in range(2)]
        nat_ps, max_sb = sem("nat_ps"), sem("max_sb")
        nm_sb, nmp1, nmr1, nmp2, nmp3 = (sem(n) for n in ("nm_sb", "nmp1", "nmr1", "nmp2", "nmp3"))
        nmT_ps, nmT_sb = sem("nmT_ps"), sem("nmT_sb")
        max_in = [sem(f"max_in{n}") for n in range(2)]
        trn_ps, exp_sb, sel_sb, av_ps = sem("trn_ps"), sem("exp_sb"), sem("sel_sb"), sem("av_ps")
        oT_sb, o_ps, rsum_sb, cn_sb = sem("oT_sb"), sem("o_ps"), sem("rsum_sb"), sem("cn_sb")
        cT_ps, cT_sb, proj_ps, h2_sb = sem("cT_ps"), sem("cT_sb"), sem("proj_ps"), sem("h2_sb")
        st2, mv2_sb, pool_var2, rstd2_sb, z3_sb = (sem(n) for n in ("st2", "mv2_sb", "pool_var2", "rstd2_sb", "z3_sb"))
        z3T_ps, z3T_sb, lg_ps, lg_sb = (sem(n) for n in ("z3T_ps", "z3T_sb", "lg_ps", "lg_sb"))
        lmax_sb, ldiff_sb, lexp_sb, lsum_sb, gate_sb = (sem(n) for n in ("lmax_sb", "ldiff_sb", "lexp_sb", "lsum_sb", "gate_sb"))
        hit_sb, first_sb, onehot_sb = sem("hit_sb"), sem("first_sb"), sem("onehot_sb")
        rank_ps, pos_sb, slots_moved, own_sb, slotf_sb, slot_sb = (sem(n) for n in ("rank_ps", "pos_sb", "slots_moved", "own_sb", "slotf_sb", "slot_sb"))
        id_sb, token_moved = sem("id_sb"), sem("token_moved")
        scattered = [sem(f"scattered{n}") for n in range(4)]
        s_plan = sem("s_plan")
        s_tail = sem("s_tail")
        b1T_ps, b1T_sb, expert_sb, y_half = sem("b1T_ps"), sem("b1T_sb"), sem("expert_sb"), sem("y_half")
        passed_waits = sem("passed_waits")
        s_plan2 = sem("s_plan2")
        s_ptail = sem("s_ptail")
        pad_in = sem("pad_in")
        tail_in = sem("tail_in")
        t_in = [sem(f"t_in{n}") for n in range(RING)]
        tT_ps, tT_sb, hid_ps, hid_sb, y_ps, y_sb = (
            sem(n) for n in ("tT_ps", "tT_sb", "hid_ps", "hid_sb", "y_ps", "y_sb"))
        y_out = [sem(f"y_out{n}") for n in range(4)]

        class Row:

            def __init__(self, k, r, unroll=UNROLL):
                self.k, self.r, self.unroll = k, r, unroll
                self.n = unroll * k + r
                self.ap = bass.ds(self.n, 1)

            def lag(self, d):
                return Row(self.k, self.r - d, self.unroll)

            def live(self, rows=NB):
                return not isinstance(self.k, int) or 0 <= self.n < rows

        def wait_apart(eng):
            eng.sem_inc(passed_waits, 1)

        def wait(eng, s, b, per=1, upto=None, rows=NB):
            upto = per if upto is None else upto
            if isinstance(b.k, int):
                n, upto = (b.n, upto) if b.n < rows else (rows - 1, per)
                if per * n + upto > 0:
                    eng.wait_ge(s, per * n + upto)
            else:
                eng.wait_ge(s, b.k * (per * b.unroll) + (per * b.r + upto))
                if eng is nc.sync:
                    wait_apart(eng)

        def wait_dma(eng, ring, b, dmas=1, rows=NB):
            m = len(ring)
            if isinstance(b.k, int):
                if b.n >= 0:
                    eng.wait_ge(ring[b.n % m], 16 * dmas * (b.n // m + 1))
            else:
                eng.wait_ge(ring[b.r % m], b.k * (16 * dmas * b.unroll // m) + 16 * dmas * (b.r // m + 1))
                if eng is nc.sync:
                    wait_apart(eng)

        def split(c, n):
            return parts[:, c, 2 - n:4 + n:1 + 2 * n, :]

        def bass_diag(a):
            return bass.AP(a.tensor, a.offset, [list(a.ap[0]), [T, 2], [1, HALF]])

        def pipeline(eng, step):
            start = LAST + 3
            loops = (NB - 2 - start) // UNROLL
            for i in range(start):
                step(Row(0, i))
            with eng.Fori(1, 1 + loops) as k:
                for j in range(UNROLL):
                    step(Row(k, start - UNROLL + j))
            for i in range(start + loops * UNROLL, NB + LAST):
                step(Row(0, i))

        def pipeline_b(eng, step, upto, lag=0):
            start = RING
            loops = (TILES - start) // RING
            for t in range(start):
                if t >= lag:
                    step(Row(0, t - lag, RING))
            with eng.Fori(0, loops) as k:
                for j in range(RING):
                    step(Row(k, start + j - lag, RING))
            for t in range(start + loops * RING, TILES + upto):
                step(Row(0, t - lag, RING))

        def fill_tails(eng, first):
            eng.wait_ge(s_tail, 1)
            for e in range(first, E, 2):
                end = eng.value_load(tail_i[0:1, e:e + 1], min_val=e * BIN, max_val=e * BIN + TOKENS)
                eng.dma_start(bins[bass.ds(end, 128), :], blank[:]).then_inc(tail_in, 16)

        block = ctx.enter_context(nc.Block())

        @block.sync
        def _(sp):
            for dst, src in (
                (tok_w_sb[:], tok_w.rearrange("(k f) u -> f k u", k=TAPS)),
                (tok_b_sb[:], tok_b.rearrange("(a u) -> a u", a=1).partition_broadcast(128)),
                (w_qkv_sb[:], w_qkv),
                (gamma_sb[:], gamma.rearrange("(p a) -> p a", a=1)),
                (beta_sb[:], beta.rearrange("(p a) -> p a", a=1)),
                (w_out_sb[:], w_out),
                (b_out_sb[:], b_out.rearrange("(a u) -> a u", a=1)),
                (w_r_sb[:, 0:E], w_r),
                (b_r_sb[:], b_r.rearrange("(a u) -> a u", a=1).partition_broadcast(128)),
            ):
                sp.dma_start(dst, src).then_inc(loads, 16)

            def load_x(b):
                wait(sp, xT_ps, b.lag(4))
                sp.dma_start(xt[:, b.r % 4, :, :], x[b.n].rearrange("(c p) f -> p c f", p=128)).then_inc(x_in[b.r % 4], 16)

            load_x(Row(0, 0))
            load_x(Row(0, 1))
            sp.wait_ge(s_const, 1)
            sp.dma_start(bins[E * BIN:E * BIN + 128, :], blank[:]).then_inc(pad_in, 16)

            def step(i):
                b = i.lag(-2)
                if b.live():
                    load_x(b)
                b = i.lag(1)
                if b.live():
                    d = b.r % 2
                    wait(sp, part3, b)
                    wait_dma(sp, stack_in, b.lag(2), dmas=len(STACKS))
                    sp.dma_start(splits[d].rearrange("s p t -> p s t"), parts[:, d]).then_inc(split_out[d], 16)
                b = i.lag(3)
                if b.live():
                    wait(sp, nmT_sb, b)
                    wait(sp, trn_ps, b.lag(4), per=HEADS)
                    sp.dma_start(Q[ROWS:MROWS, b.r % 4], nmaxT[:, b.r % 2, :]).then_inc(max_in[b.r % 2], 16)
                b = i.lag(1)
                if b.live():
                    d, c = b.r % 2, b.r % 4
                    wait_dma(sp, split_out, b)
                    wait(sp, trn_ps, b.lag(4), per=HEADS)
                    for operand, first_row, where, which in STACKS:
                        rows = bass.AP(splits.tensor, splits[d, where].offset,
                                       [[step * HEADS * T, n] for step, n in which] + [[1, HEADS * T]])
                        last_row = first_row + which[0][1] * which[1][1]
                        sp.dma_start((Q, K)[operand][first_row:last_row, c].rearrange("p h t -> p (h t)"),
                                     rows).then_inc(stack_in[d], 16)
                if isinstance(i.k, int) and i.n == 2:
                    for dst, src in (
                        (experts[:, :, 0:D], w_1.rearrange("e h f -> h e f")),
                        (experts[:, :, D:2 * D], w_2.rearrange("e h f -> h e f")),
                        (b_1_rows[:], b_1),
                        (b_2_sb[:], b_2.rearrange("(a e) f -> a e f", a=1).partition_broadcast(128)),
                    ):
                        sp.dma_start(dst, src).then_inc(loads, 16)

            pipeline(sp, step)

            fill_tails(sp, 0)
            for n in range(4):
                sp.wait_ge(scattered[n], 16 * 2 * NB // 4)
            sp.wait_ge(tail_in, 16 * E)
            sp.wait_ge(pad_in, 16)
            sp.wait_ge(s_plan, 1)

            def step_b(t):
                b = t.lag(RING)
                if not (isinstance(b.k, int) and b.n < 0):
                    wait_dma(sp, y_out, b, rows=TILES)
                row = sp.value_load(row_i[0:1, bass.ds(t.n, 1)], min_val=0, max_val=PAD_TILE)
                sp.dma_start(tile_in[:, t.r % RING, :], bins[bass.ds(row * 128, 128), :]).then_inc(t_in[t.r % RING], 16)

            pipeline_b(sp, step_b, upto=0)
            for n in range(4):
                sp.wait_ge(y_out[n], 16 * len(range(n, TILES, 4)))

        @block.gpsimd
        def _(pool):
            g = nc.gpsimd
            chain = [0]

            def link(ins):
                chain[0] += 1
                ins.then_inc(s_chain, 1)
                pool.wait_ge(s_chain, chain[0])

            link(g.memset(blank[:, 0:IDCOL], 0.0))
            link(g.memset(blank[:, IDCOL:REC].bitcast(I32), NO_TOKEN))
            link(g.memset(K[ROWS:MROWS], 1.0))
            link(g.memset(w_r_sb[:, E:D], 0.0))
            link(g.memset(ident[:], 1.0))
            link(g.memset(causal[:], 0.0))
            link(g.memset(before[:], 1.0))
            link(g.memset(ones_bf[:], 1.0))
            link(g.memset(ones_row[:], 1.0))
            link(g.memset(neg_half[:], -0.5))
            link(g.memset(one_e[:], 1.0))
            link(g.memset(V[:], 0.0))
            link(g.memset(V[:, :, :, :, HD:HD + 1], 1.0))
            link(g.affine_select(out=ident[:], in_=ident[:], compare_op=ALU.is_equal, fill=0.0, base=0,
                                 pattern=[[-1, 128]], channel_multiplier=1))
            link(g.tensor_copy(ident_bf[:], ident[:]))
            link(g.affine_select(out=causal[:], in_=causal[:], compare_op=ALU.is_ge, fill=NEG, base=0,
                            pattern=[[0, 2], [-1, HALF]], channel_multiplier=1))
            link(g.affine_select(out=before[:], in_=before[:], compare_op=ALU.is_gt, fill=0.0, base=0,
                            pattern=[[1, HALF]], channel_multiplier=-1))
            link(g.iota(iota_i[:, 0:E], [[BIN, E]], base=0, channel_multiplier=0))
            link(g.iota(iota_i[:, E:2 * E], [[-1, E]], base=E, channel_multiplier=0))
            link(g.iota(token_i[:], [[HALF, 2]], base=0, channel_multiplier=1))
            link(g.iota(tile_no_i[:], [[1, TILES]], base=0, channel_multiplier=0))
            link(g.tensor_copy(bin_start[:], iota_i[:, 0:E]))
            link(g.tensor_copy(next_slot[:], iota_i[:, 0:E]))
            link(g.tensor_copy(rank_weight[:], iota_i[:, E:2 * E]))
            link(g.tensor_copy(token[:], token_i[:]))
            g.tensor_copy(tile_no[:], tile_no_i[:]).then_inc(s_const, 1)
            pool.wait_ge(s_const, 1)

            def keep_causal(b, hd):
                wait(pool, exp_sb, b, per=HEADS, upto=hd + 1)
                wait_apart(pool)
                v = P[0:HALF, hd, :]
                diag = bass_diag(v)
                g.affine_select(out=diag, in_=diag, compare_op=ALU.is_ge, fill=0.0, base=0,
                                pattern=[[0, 2], [1, HALF]], channel_multiplier=-1).then_inc(sel_sb, 1)

            def norm_factors(b):
                c = b.r % 2
                wait(pool, mv_sb, b)
                wait(pool, z_sb, b.lag(2), per=2)
                wait(pool, base_part, b.lag(1), per=2)
                wait_apart(pool)
                g.tensor_scalar(var_e[0:HALF, 0:2], mv[0:HALF, c, :, 1], 1.0, EPS, ALU.mult, ALU.add)
                g.tensor_scalar(neg_m[0:HALF], mv[0:HALF, c, :, 0], -1.0, 0.0, ALU.mult, ALU.add)
                g.tensor_scalar(var_e[0:HALF, 2:4], mv[0:HALF, c, :, 1], 1.0 + EPS, EPS * EPS, ALU.mult,
                                ALU.add).then_inc(pool_var, 1)
                wait(pool, pool_var, b)
                g.tensor_tensor(rstd[0:HALF, c, :], var_e[0:HALF], neg_half[0:HALF], ALU.pow).then_inc(pool_rstd, 1)
                wait(pool, pool_rstd, b)
                g.tensor_tensor(neg_mr[0:HALF], neg_m[0:HALF], rstd[0:HALF, c, 0:2], ALU.mult)
                g.tensor_scalar(one_r[0:HALF], rstd[0:HALF, c, 0:2], 1.0, 1.0, ALU.mult, ALU.add).then_inc(pool_sc, 1)

            def add_bias(b):
                wait(pool, base_part, b, per=2)
                g.tensor_tensor(base[0:HALF, b.ap, :, :].rearrange("p a c u -> p (a c u)"),
                                base_h[0:HALF].rearrange("p c u -> p (c u)"),
                                o_bias[0:HALF].rearrange("p c u -> p (c u)"), ALU.add).then_inc(base_sb, 1)

            def norm_factor2(b):
                c = b.r % 2
                wait(pool, mv2_sb, b)
                wait(pool, z3_sb, b.lag(2), per=2)
                wait_apart(pool)
                g.tensor_scalar(var2_e[0:HALF], mv2[0:HALF, c, :, 1], 1.0, EPS, ALU.mult, ALU.add).then_inc(pool_var2, 1)
                wait(pool, pool_var2, b)
                g.tensor_tensor(rstd2[0:HALF, c, :], var2_e[0:HALF], neg_half[0:HALF, 0:2], ALU.pow).then_inc(rstd2_sb, 1)

            def scatter(b, n):
                c = b.r % 4
                if n == 0:
                    wait(pool, slot_sb, b)
                    wait(pool, gate_sb, b)
                    wait(pool, id_sb, b)
                    wait(pool, z3_sb, b, per=2)
                    wait_apart(pool)
                g.indirect_dma_start(bins, bass.IndirectOffsetOnAxis(ap=slot[0:HALF, c, n:n + 1], axis=0),
                                     rec[0:HALF, c, n, :], None, bounds_check=E * BIN - 1,
                                     oob_is_err=False).then_inc(scattered[b.r % 4], 16)

            pool.wait_ge(s_setup, 1)

            def step(i):
                b, r, q = i.lag(4), i.lag(6), i.lag(7)
                for hd in range(HEADS):
                    if hd == 3 and i.live():
                        norm_factors(i)
                    if b.live():
                        keep_causal(b, hd)
                    if hd == 0 and r.live():
                        norm_factor2(r)
                    if hd == 2 and q.live():
                        scatter(q, 0)
                    if hd == 5 and q.live():
                        scatter(q, 1)
                    if hd == 6 and i.live():
                        add_bias(i)

            pipeline(pool, step)

            def step_b(t):
                c = t.r % 4
                wait(pool, y_sb, t, rows=TILES)
                wait_apart(pool)
                g.indirect_dma_start(out.rearrange("b t u -> (b t) u"),
                                     bass.IndirectOffsetOnAxis(ap=tile_in[:, t.r % RING, IDCOL:REC].bitcast(I32), axis=0),
                                     y[:, c, :], None, bounds_check=TOKENS - 1,
                                     oob_is_err=False).then_inc(y_out[c], 16)

            pipeline_b(pool, step_b, upto=3, lag=3)

        @block.scalar
        def _(act):
            a = nc.scalar

            def exp_scores(b, hd):
                wait(act, trn_ps, b, per=HEADS, upto=hd + 1)
                wait(act, av_ps, b.lag(1), per=HEADS, upto=hd + 1)
                a.activation(P[0:HALF, hd, :], ps[0:HALF, TRN + hd % 2, 0:TRI], ACT.Exp).then_inc(exp_sb, 1)

            def xT_copy(b):
                wait(act, xT_ps, b)
                wait(act, conv_ps, b.lag(2))
                a.copy(xT[:, b.r % 2, :], ps[:, M0, 0:TIN]).then_inc(xT_sb, 1)

            def zT_copy(b):
                wait(act, zT_ps, b)
                wait(act, v_ps, b.lag(2))
                a.copy(zT[:, b.r % 2, :], ps[:, M1, 0:T]).then_inc(zT_sb, 1)

            def qk_copy(b):
                c = b.r % 2
                wait(act, qk_ps, b)
                wait(act, rest1, b.lag(2))
                for n in range(2):
                    a.activation(qk[:, c, n, :], ps[:, M1, n * T:(n + 1) * T], ACT.Identity,
                                 bias=qk_bias[:, n:n + 1]).then_inc(qk_sb, 1)
                wait(act, qk_sb, b, per=2)
                wait_dma(act, split_out, b.lag(2))
                a.copy(split(c, 0), qk[:, c]).then_inc(part1, 1)

            def second_parts(b):
                wait(act, rest1, b)
                a.copy(split(b.r % 2, 1), rest[:, b.r % 2]).then_inc(part2, 1)

            def v_copy(b):
                wait(act, v_ps, b)
                wait(act, av_ps, b.lag(4), per=HEADS)
                a.copy(V[0:HALF, b.r % 4, :, :, 0:HD].rearrange("p c h d -> p (c h) d"),
                       ps[0:HALF, M0, 0:2 * D].rearrange("p (c d) -> p c d", d=HD)).then_inc(v_sb, 1)

            def nmaxT_copy(b):
                wait(act, nmT_ps, b)
                wait_dma(act, max_in, b.lag(2))
                a.copy(nmaxT[:, b.r % 2, :], ps[0:PARTS * HEADS, MID, 0:T // 2 + 0].bitcast(BF16)[:, 0:T]).then_inc(nmT_sb, 1)

            def oT_copy(b):
                wait(act, av_ps, b, per=HEADS)
                wait(act, o_ps, b.lag(1))
                a.copy(oT[:], ps[:, AV, 0:2 * T].rearrange("p (c t) -> p c t", c=2)).then_inc(oT_sb, 1)

            def cT_copy(b):
                wait(act, cT_ps, b)
                wait(act, proj_ps, b.lag(2))
                a.copy(cT[:, b.r % 2, :], ps[:, M0, 0:T]).then_inc(cT_sb, 1)

            def z3T_copy(b):
                wait(act, z3T_ps, b)
                wait(act, lg_ps, b.lag(2))
                a.copy(z3T[:, b.r % 2, :], ps[:, M0, 0:T]).then_inc(z3T_sb, 1)

            def residual(b):
                c = b.r % 2
                wait(act, pool_sc, b)
                wait(act, base_sb, b.lag(1))
                for n in range(2):
                    a.activation(base_h[0:HALF, n], h[0:HALF, c, n], ACT.Identity, bias=neg_mr[0:HALF, n:n + 1],
                                 scale=one_r[0:HALF, n:n + 1]).then_inc(base_part, 1)

            def logit_exp(b):
                wait(act, ldiff_sb, b)
                wait(act, lsum_sb, b.lag(2))
                a.activation(lexp[0:HALF, b.r % 2], ldiff[0:HALF, b.r % 2], ACT.Exp).then_inc(lexp_sb, 1)

            act.wait_ge(s_setup, 1)
            act.wait_ge(s_const, 1)
            xT_copy(Row(0, 0))

            def step(i):
                s, b, u, r = i.lag(3), i.lag(4), i.lag(5), i.lag(6)
                for hd in range(HEADS):
                    if hd == 2:
                        if s.live():
                            nmaxT_copy(s)
                        if u.live():
                            oT_copy(u)
                    if hd == 3 and i.lag(1).live():
                        v_copy(i.lag(1))
                    if hd == 4 and r.live():
                        z3T_copy(r)
                    if hd == 5 and i.lag(-1).live():
                        xT_copy(i.lag(-1))
                    if hd == 6:
                        if u.live():
                            cT_copy(u)
                        if i.live():
                            zT_copy(i)
                    if hd == 7 and i.live():
                        qk_copy(i)
                    if b.live():
                        exp_scores(b, hd)
                    if hd == 0 and i.lag(1).live():
                        second_parts(i.lag(1))
                    if hd == 5 and i.live():
                        residual(i)
                    if hd == 6 and r.live():
                        logit_exp(r)

            pipeline(act, step)

            fill_tails(act, 1)
            act.wait_ge(b1T_sb, 1)

            def step_b(t):
                if t.live(TILES):
                    wait(act, tT_ps, t, rows=TILES)
                    wait(act, hid_ps, t.lag(2), rows=TILES)
                    a.copy(tT[:, t.r % 2, :], ps[:, 0 + t.r % 2, 0:128]).then_inc(tT_sb, 1)
                b = t.lag(1)
                if b.live(TILES):
                    wait(act, hid_ps, b, rows=TILES)
                    wait(act, y_ps, b.lag(2), rows=TILES)
                    a.activation(hidT[:, b.r % 2, :], ps[:, 2 + b.r % 2, 0:128], ACT.Relu,
                                 bias=expert[:, b.r % 4, 2 * D:W_COLS]).then_inc(hid_sb, 1)

            pipeline_b(act, step_b, upto=1)

        @block.vector
        def _(dve):
            v = nc.vector
            dve.wait_ge(loads, 16 * 9)
            for n in range(2):
                v.tensor_copy(w_raw[:, n, :].rearrange("p (d h) -> p d h", h=HEADS),
                              w_qkv_sb[:, n * D:(n + 1) * D].rearrange("p (h d) -> p d h", h=HEADS)).then_inc(s_setup_pe, 1)
            scale = float(HD) ** -0.5
            v.tensor_scalar(gamma_q[:], gamma_sb[:], scale, None, ALU.mult).then_inc(s_setup_pe, 1)
            dve.wait_ge(s_setup_pe, 3)
            v.tensor_scalar(w_q[:], w_raw[:, 0, :], gamma_q[:, 0:1], None, ALU.mult)
            v.tensor_scalar(w_k[:], w_raw[:, 1, :], gamma_sb[:, 0:1], None, ALU.mult)
            v.tensor_scalar(w_v[:], w_qkv_sb[:, 2 * D:3 * D], gamma_sb[:, 0:1], None, ALU.mult)
            dve.wait_ge(s_ptail, 1)
            v.tensor_scalar(qk_bias[:, 0:1], ps[:, 4, 0:1], scale, None, ALU.mult)
            v.tensor_copy(qk_bias[:, 1:2], ps[:, 4, 1:2])
            v.tensor_copy(v_bias[:], ps[:, 4, 2:3]).then_inc(s_setup_pe, 1)
            dve.wait_ge(s_ptail, 2)
            v.tensor_tensor(o_bias_row[:], ps[0:1, 5, 0:D], b_out_sb[:], ALU.add).then_inc(s_setup_pe, 1)
            dve.wait_ge(s_ptail, 3)
            v.tensor_copy(o_bias[:, 0, :], ps[:, 4, 0:D])
            v.tensor_copy(o_bias[:, 1, :], ps[:, 4, 0:D]).then_inc(s_setup, 1)
            dve.wait_ge(s_const, 1)

            def row_max(b, hd):
                wait(dve, nat_ps, b, per=HEADS, upto=hd + 1)
                v.tensor_reduce(nmax3[0:HALF, b.r % 2, hd, :],
                                ps[0:HALF, NAT + hd % 2, 0:TRI].rearrange("p (c s) -> p c s", c=3),
                                AX.X, ALU.max, negate=True).then_inc(max_sb, 1)

            def negate_max(b):
                c = b.r % 2
                wait(dve, max_sb, b, per=HEADS)
                v.tensor_copy(nmax[0:HALF, 0, :], nmax3[0:HALF, c, :, 0])
                v.tensor_tensor(nmax[0:HALF, 1, :], nmax3[0:HALF, c, :, 1], nmax3[0:HALF, c, :, 2], ALU.min).then_inc(nm_sb, 1)

            def max_part0(b):
                wait(dve, nm_sb, b)
                wait(dve, nmT_ps, b.lag(2))
                v.tensor_copy(nmax_parts[0:HALF, b.r % 2, :, 0, :], nmax[0:HALF]).then_inc(nmp1, 1)

            def max_rest(b):
                wait(dve, nmp1, b)
                v.tensor_tensor(nmax_rest[0:HALF], nmax[0:HALF], nmax_parts[0:HALF, b.r % 2, :, 0, :], ALU.subtract).then_inc(nmr1, 1)

            def max_part1(b):
                wait(dve, nmr1, b)
                v.tensor_copy(nmax_parts[0:HALF, b.r % 2, :, 1, :], nmax_rest[0:HALF]).then_inc(nmp2, 1)

            def max_part2(b):
                wait(dve, nmp2, b)
                v.tensor_tensor(nmax_parts[0:HALF, b.r % 2, :, 2, :], nmax_rest[0:HALF], nmax_parts[0:HALF, b.r % 2, :, 1, :],
                                ALU.subtract).then_inc(nmp3, 1)

            def third_parts(b):
                wait(dve, part2, b)
                v.tensor_tensor(split(b.r % 2, 2), rest[:, b.r % 2], split(b.r % 2, 1),
                                ALU.subtract).then_inc(part3, 1)

            def first_rest(b):
                c = b.r % 2
                wait(dve, part1, b)
                wait(dve, part3, b.lag(2))
                v.tensor_tensor(rest[:, c], qk[:, c], split(c, 0), ALU.subtract).then_inc(rest1, 1)

            def tokens(b):
                wait(dve, conv_ps, b)
                wait(dve, base_part, b.lag(2), per=2)
                v.tensor_tensor(h[0:HALF, b.r % 2], ps[0:HALF, M1, 0:2 * D].rearrange("p (c u) -> p c u", c=2),
                                tok_b_sb[0:HALF, None, :].to_broadcast([HALF, 2, D]), ALU.add).then_inc(h_sb, 1)

            def token_stats(b):
                wait(dve, h_sb, b)
                for n in range(2):
                    v.bn_stats(stats[0:HALF, n, :], h[0:HALF, b.r % 2, n, :]).then_inc(st1, 1)

            def token_moments(b):
                c = b.r % 2
                wait(dve, st1, b, per=2)
                wait_apart(dve)
                v.bn_aggr(mv[0:HALF, c, 0, :], stats[0:HALF, 0, :])
                v.bn_aggr(mv[0:HALF, c, 1, :], stats[0:HALF, 1, :]).then_inc(mv_sb, 1)

            def normalise(b, n):
                c = b.r % 2
                if n == 0:
                    wait(dve, pool_rstd, b)
                    wait(dve, zT_ps, b.lag(2))
                v.tensor_scalar(z[0:HALF, c, n], h[0:HALF, c, n], mv[0:HALF, c, n, 0:1],
                                rstd[0:HALF, c, 2 + n:3 + n], ALU.subtract, ALU.mult).then_inc(z_sb, 1)

            def prob_sums(b):
                wait(dve, o_ps, b)
                o = ps[0:HALF, MID, :].rearrange("p (g c) -> p g c", c=32)
                v.reciprocal(rsum[0:HALF], o[:, :, HD]).then_inc(rsum_sb, 1)

            def divide(b):
                wait(dve, rsum_sb, b)
                wait(dve, cT_ps, b.lag(2))
                o = ps[0:HALF, MID, :].rearrange("p (g c) -> p g c", c=32)
                v.tensor_tensor(cn[0:HALF, b.r % 2].rearrange("p c (h d) -> p (c h) d", d=HD), o[:, :, 0:HD],
                                rsum[0:HALF, :, None].to_broadcast([HALF, 16, HD]), ALU.mult).then_inc(cn_sb, 1)

            def residual(b):
                wait(dve, proj_ps, b)
                wait(dve, base_sb, b)
                wait_dma(dve, scattered, b.lag(4), dmas=2)
                v.tensor_tensor(rec[0:HALF, b.r % 4, :, D:2 * D], ps[0:HALF, M0, 0:2 * D].rearrange("p (c u) -> p c u", c=2),
                                base[0:HALF, b.ap, :, :].rearrange("p a c u -> p (a c) u"), ALU.add).then_inc(h2_sb, 1)

            def residual_stats(b):
                wait(dve, h2_sb, b)
                for n in range(2):
                    v.bn_stats(stats2[0:HALF, n, :], rec[0:HALF, b.r % 4, n, D:2 * D]).then_inc(st2, 1)

            def residual_moments(b):
                c = b.r % 2
                wait(dve, st2, b, per=2)
                wait_apart(dve)
                v.bn_aggr(mv2[0:HALF, c, 0, :], stats2[0:HALF, 0, :])
                v.bn_aggr(mv2[0:HALF, c, 1, :], stats2[0:HALF, 1, :]).then_inc(mv2_sb, 1)

            def normalise2(b):
                c = b.r % 2
                wait(dve, rstd2_sb, b)
                for n in range(2):
                    v.tensor_scalar(rec[0:HALF, b.r % 4, n, 0:D], rec[0:HALF, b.r % 4, n, D:2 * D], mv2[0:HALF, c, n, 0:1],
                                    rstd2[0:HALF, c, n:n + 1], ALU.subtract, ALU.mult).then_inc(z3_sb, 1)

            def logit_bias(b):
                wait(dve, lg_ps, b)
                v.tensor_tensor(lg[0:HALF], ps[0:HALF, M1, 0:2 * D].rearrange("p (c u) -> p c u", c=2)[:, :, 0:E],
                                b_r_sb[0:HALF, None, :].to_broadcast([HALF, 2, E]), ALU.add).then_inc(lg_sb, 1)

            def logit_max(b):
                wait(dve, lg_sb, b)
                v.tensor_reduce(lmax[0:HALF], lg[0:HALF], AX.X, ALU.max).then_inc(lmax_sb, 1)

            def logit_diff(b):
                wait(dve, lmax_sb, b)
                wait(dve, lexp_sb, b.lag(2))
                v.tensor_tensor(ldiff[0:HALF, b.r % 2], lg[0:HALF], lmax[0:HALF, :, None].to_broadcast([HALF, 2, E]),
                                ALU.subtract).then_inc(ldiff_sb, 1)

            def hits(b):
                wait(dve, ldiff_sb, b)
                v.scalar_tensor_tensor(hit[0:HALF], ldiff[0:HALF, b.r % 2], 0.0,
                                       rank_weight[0:HALF, None, :].to_broadcast([HALF, 2, E]),
                                       ALU.is_equal, ALU.mult).then_inc(hit_sb, 1)

            def first_hit(b):
                wait(dve, hit_sb, b)
                v.tensor_reduce(first[0:HALF], hit[0:HALF], AX.X, ALU.max).then_inc(first_sb, 1)

            def one_expert(b):
                wait(dve, first_sb, b)
                wait(dve, rank_ps, b.lag(2))
                v.tensor_tensor(onehot[0:HALF, b.r % 2], hit[0:HALF], first[0:HALF, :, None].to_broadcast([HALF, 2, E]),
                                ALU.is_equal).then_inc(onehot_sb, 1)

            def record_id(b):
                v.tensor_copy(rec[0:HALF, b.r % 4, :, IDCOL].bitcast(I32), token[0:HALF]).then_inc(id_sb, 1)
                v.tensor_scalar(token[0:HALF], token[0:HALF], float(T), None, ALU.add).then_inc(token_moved, 1)

            def exp_sum(b):
                wait(dve, lexp_sb, b)
                v.tensor_reduce(lsum[0:HALF], lexp[0:HALF, b.r % 2], AX.X, ALU.add).then_inc(lsum_sb, 1)

            def record_gate(b):
                wait(dve, lsum_sb, b)
                v.reciprocal(rec[0:HALF, b.r % 4, :, GATE], lsum[0:HALF]).then_inc(gate_sb, 1)

            def positions(b):
                wait(dve, rank_ps, b)
                wait(dve, slots_moved, b.lag(1))
                v.tensor_tensor(pos[0:HALF], ps[0:HALF, MID, 0:2 * E].rearrange("p (c e) -> p c e", e=E),
                                next_slot[0:HALF, None, :].to_broadcast([HALF, 2, E]), ALU.add).then_inc(pos_sb, 1)

            def own_position(b):
                wait(dve, pos_sb, b)
                v.tensor_tensor(next_slot[0:HALF], ps[0:HALF, MID, 2 * E:3 * E], next_slot[0:HALF], ALU.add).then_inc(slots_moved, 1)
                v.tensor_tensor(pos_own[0:HALF], pos[0:HALF], onehot[0:HALF, b.r % 2], ALU.mult).then_inc(own_sb, 1)

            def slot_sum(b):
                wait(dve, own_sb, b)
                v.tensor_reduce(slot_f[0:HALF], pos_own[0:HALF], AX.X, ALU.add).then_inc(slotf_sb, 1)

            def slot_number(b):
                wait(dve, slotf_sb, b)
                v.tensor_copy(slot[0:HALF, b.r % 4, :], slot_f[0:HALF]).then_inc(slot_sb, 1)

            def step(i):
                j, n, s, u, r, q = i.lag(1), i.lag(2), i.lag(3), i.lag(5), i.lag(6), i.lag(7)

                def turn(*work):
                    for stage, b, *rest_of in work:
                        if b.live():
                            stage(b, *rest_of)

                turn((negate_max, s), (positions, q), (max_part0, s), (own_position, q), (max_rest, s), (slot_sum, q),
                     (max_part1, s), (slot_number, q), (max_part2, s), (row_max, n, 0))
                turn((row_max, n, 1), (third_parts, j), (normalise2, r))
                turn((row_max, n, 2), (tokens, i), (token_stats, i))
                turn((row_max, n, 3), (token_moments, i))
                turn((row_max, n, 4), (prob_sums, u), (logit_bias, r), (divide, u), (logit_max, r), (normalise, i, 0),
                     (logit_diff, r), (normalise, i, 1))
                turn((row_max, n, 5), (hits, r), (record_id, r))
                turn((first_hit, r), (row_max, n, 6), (one_expert, r), (exp_sum, r))
                turn((residual, u), (row_max, n, 7), (record_gate, r), (residual_stats, u), (first_rest, i), (residual_moments, u))

            pipeline(dve, step)

            chain = [0]

            def link(ins):
                chain[0] += 1
                ins.then_inc(s_plan2, 1)
                dve.wait_ge(s_plan2, chain[0])

            dve.wait_ge(slots_moved, NB)
            v.tensor_copy(tail_i[:], next_slot[0:1]).then_inc(s_tail, 1)
            dve.wait_ge(b1T_ps, 1)
            v.tensor_copy(experts[:, :, 2 * D], ps[:, 0, 0:E]).then_inc(b1T_sb, 1)
            link(v.tensor_tensor(count[:], next_slot[0:1], bin_start[0:1], ALU.subtract))
            link(v.tensor_scalar(count[:], count[:], 127.0, None, ALU.add))
            link(v.tensor_copy(count_i[:], count[:]))
            link(v.tensor_scalar(tiles_i[:], count_i[:], 7, None, ALU.logical_shift_right))
            link(v.tensor_copy(tiles_f[:], tiles_i[:]))
            link(v.tensor_tensor_scan(tiles_end[:], one_e[:], tiles_f[:], 0.0, ALU.mult, ALU.add))
            link(v.tensor_tensor(passed[:], tiles_end[:, None, :].to_broadcast([1, TILES, E]),
                                 tile_no[:, :, None].to_broadcast([1, TILES, E]), ALU.is_le))
            link(v.tensor_reduce(expert_f[:], passed[:], AX.X, ALU.add))
            link(v.tensor_tensor(skipped[:], passed[:], tiles_f[:, None, :].to_broadcast([1, TILES, E]), ALU.mult))
            link(v.tensor_reduce(start_f[:], skipped[:], AX.X, ALU.add))
            link(v.tensor_tensor(row_f[:], tile_no[:], start_f[:], ALU.subtract))
            link(v.tensor_scalar(row_a[:], expert_f[:], float(BIN // 128), None, ALU.mult))
            link(v.tensor_tensor(row_b[:], row_a[:], row_f[:], ALU.add))
            link(v.tensor_scalar(row_a[:], row_b[:], float(PAD_TILE), None, ALU.min))
            link(v.tensor_scalar(expert_c[:], expert_f[:], float(E - 1), None, ALU.min))
            link(v.tensor_copy(row_i[:], row_a[:]))
            v.tensor_copy(expert_i[:], expert_c[:]).then_inc(s_plan, 1)
            dve.wait_ge(s_plan, 1)
            dve.wait_ge(b1T_sb, 1)

            def step_b(t):
                if t.live(TILES):
                    e = dve.value_load(expert_i[0:1, bass.ds(t.n, 1)], min_val=0, max_val=E - 1)
                    wait(dve, y_ps, t.lag(4), rows=TILES)
                    v.tensor_copy(expert[:, t.r % 4, :], experts[:, bass.ds(e, 1), :].rearrange("p a c -> p (a c)")).then_inc(expert_sb, 1)
                b = t.lag(2)
                if b.live(TILES):
                    e = dve.value_load(expert_i[0:1, bass.ds(b.n, 1)], min_val=0, max_val=E - 1)
                    wait(dve, y_ps, b, rows=TILES)
                    wait(dve, y_sb, b.lag(2), rows=TILES)
                    v.tensor_tensor(y_part[:, b.r % 2, :], ps[:, 6 + b.r % 2, 0:D],
                                    b_2_sb[:, bass.ds(e, 1), :].rearrange("p a c -> p (a c)"), ALU.add).then_inc(y_half, 1)
                b = t.lag(3)
                if b.live(TILES):
                    wait(dve, y_half, b, rows=TILES)
                    u = b.lag(4)
                    if not (isinstance(u.k, int) and u.n < 0):
                        wait_dma(dve, y_out, u, rows=TILES)
                    v.scalar_tensor_tensor(y[:, b.r % 4, :], y_part[:, b.r % 2, :], tile_in[:, b.r % RING, GATE:GATE + 1],
                                           tile_in[:, b.r % RING, D:2 * D], ALU.mult, ALU.add).then_inc(y_sb, 1)

            pipeline_b(dve, step_b, upto=3)

        @block.tensor
        def _(pe):
            mm, tp = nc.tensor.matmul, nc.tensor.transpose
            pe.wait_ge(loads, 16 * 9)
            pe.wait_ge(s_setup_pe, 3)
            pe.wait_ge(s_const, 1)
            mm(ps[:, 4, 0:1], w_raw[:, 0, :], beta_sb[:], start=True, stop=True)
            mm(ps[:, 4, 1:2], w_raw[:, 1, :], beta_sb[:], start=True, stop=True)
            mm(ps[:, 4, 2:3], w_qkv_sb[:, 2 * D:3 * D], beta_sb[:], start=True, stop=True).then_inc(s_ptail, 1)
            pe.wait_ge(s_setup_pe, 4)
            mm(ps[0:1, 5, 0:D], v_bias[:], w_out_sb[:], start=True, stop=True).then_inc(s_ptail, 1)
            pe.wait_ge(s_setup_pe, 5)
            mm(ps[:, 4, 0:D], ones_row[:], o_bias_row[:], start=True, stop=True).then_inc(s_ptail, 1)
            pe.wait_ge(s_setup, 1)

            def x_transpose(b):
                wait_dma(pe, x_in, b)
                wait(pe, v_sb, b.lag(2))
                wait(pe, z3T_sb, b.lag(7))
                for n in range(2):
                    last = tp(ps[:, M0, n * 128:(n + 1) * 128], xt[:, b.r % 4, n, :], ident[:])
                last.then_inc(xT_ps, 1)

            def conv(b, n):
                if n == 0:
                    wait(pe, xT_sb, b)
                    wait(pe, qk_sb, b.lag(1), per=2)
                for k in range(TAPS):
                    last = mm(ps[0:HALF, M1, n * D:(n + 1) * D], xT[:, b.r % 2, n * HALF + k:(n + 1) * HALF + k],
                              tok_w_sb[:, k, :], start=(k == 0), stop=(k == TAPS - 1))
                if n == 1:
                    last.then_inc(conv_ps, 1)

            def z_transpose(b):
                wait(pe, z_sb, b, per=2)
                wait(pe, lg_sb, b.lag(6))
                for n in range(2):
                    last = tp(ps[:, M1, n * HALF:(n + 1) * HALF], z[0:HALF, b.r % 2, n, :], ident[0:HALF, 0:HALF])
                last.then_inc(zT_ps, 1)

            def project_qk(b):
                wait(pe, zT_sb, b)
                for n, w in enumerate((w_q, w_k)):
                    last = mm(ps[:, M1, n * T:(n + 1) * T], w[:], zT[:, b.r % 2, :], start=True, stop=True)
                last.then_inc(qk_ps, 1)

            def project_v(b):
                wait(pe, h2_sb, b.lag(5))
                wait(pe, xT_sb, b.lag(-1))
                for n in range(2):
                    last = mm(ps[0:HALF, M0, n * D:(n + 1) * D], zT[:, b.r % 2, n * HALF:(n + 1) * HALF], w_v[:],
                              start=True, stop=True)
                last.then_inc(v_ps, 1)

            def scores(b, hd):
                if hd == 0:
                    wait_dma(pe, stack_in, b, dmas=len(STACKS))
                c, bank = b.r % 4, NAT + hd % 2
                wait(pe, max_sb, b, per=HEADS, upto=hd - 1)
                mm(ps[0:HALF, bank, 0:HALF], Q[0:ROWS, c, hd, 0:HALF], K[0:ROWS, c, hd, 0:HALF], start=True, stop=False,
                   skip_group_check=True)
                mm(ps[0:HALF, bank, HALF:TRI], Q[0:ROWS, c, hd, HALF:T], K[0:ROWS, c, hd, :], start=False, stop=False,
                   skip_group_check=True)
                mm(bass_diag(ps[0:HALF, bank, 0:TRI]), ident_bf[0:HALF, 0:HALF], causal[0:HALF], start=False, stop=True,
                   skip_group_check=True).then_inc(nat_ps, 1)

            def scores_T(b, hd):
                if hd == 0:
                    wait_dma(pe, max_in, b)
                c, bank = b.r % 4, TRN + hd % 2
                wait(pe, exp_sb, b, per=HEADS, upto=hd - 1)
                mm(ps[0:HALF, bank, 0:T], K[0:MROWS, c, hd, 0:HALF], Q[0:MROWS, c, hd, :], start=True, stop=True,
                   skip_group_check=True)
                mm(ps[0:HALF, bank, T:TRI], K[0:MROWS, c, hd, HALF:T], Q[0:MROWS, c, hd, HALF:T], start=False, stop=True,
                   skip_group_check=True).then_inc(trn_ps, 1)

            def values(b, hd):
                if hd == 0:
                    wait(pe, oT_sb, b.lag(1))
                    wait(pe, v_sb, b)
                wait(pe, sel_sb, b, per=HEADS, upto=hd + 1)
                c, s, j = b.r % 4, hd // 4, 32 * (hd % 4)
                mm(ps[j:j + 32, AV, s * T:(s + 1) * T], V[0:HALF, c, 0, hd, :], P[0:HALF, hd, 0:T], start=True, stop=False,
                   skip_group_check=True)
                mm(ps[j:j + 32, AV, s * T + HALF:(s + 1) * T], V[0:HALF, c, 1, hd, :], P[0:HALF, hd, T:TRI],
                   start=False, stop=True, skip_group_check=True).then_inc(av_ps, 1)

            def max_transpose(b):
                wait(pe, nmp3, b)
                wait(pe, slots_moved, b.lag(4))
                wait(pe, cn_sb, b.lag(3))
                wait(pe, nmT_sb, b.lag(1))
                for n in range(2):
                    last = tp(ps[0:PARTS * HEADS, MID, n * HALF // 2:(n + 1) * HALF // 2].bitcast(BF16),
                              nmax_parts[0:HALF, b.r % 2, n].rearrange("p s h -> p (s h)"), ident_bf[0:HALF, 0:HALF])
                last.then_inc(nmT_ps, 1)

            def heads_transpose(b):
                wait(pe, oT_sb, b)
                wait(pe, nmT_sb, b.lag(-2))
                wait(pe, slots_moved, b.lag(2))
                for n in range(2):
                    for s in range(2):
                        last = tp(ps[0:HALF, MID, (2 * n + s) * 128:(2 * n + s + 1) * 128],
                                  oT[:, s, n * HALF:(n + 1) * HALF], ident[:])
                last.then_inc(o_ps, 1)

            def c_transpose(b):
                wait(pe, cn_sb, b)
                wait(pe, xT_sb, b.lag(-6))
                wait(pe, z3T_sb, b.lag(1))
                for n in range(2):
                    last = tp(ps[:, M0, n * HALF:(n + 1) * HALF], cn[0:HALF, b.r % 2, n, :], ident[0:HALF, 0:HALF])
                last.then_inc(cT_ps, 1)

            def project_out(b):
                wait(pe, cT_sb, b)
                for n in range(2):
                    last = mm(ps[0:HALF, M0, n * D:(n + 1) * D], cT[:, b.r % 2, n * HALF:(n + 1) * HALF], w_out_sb[:],
                              start=True, stop=True)
                last.then_inc(proj_ps, 1)

            def z3_transpose(b):
                wait(pe, z3_sb, b, per=2)
                wait(pe, v_sb, b.lag(-5))
                wait(pe, h2_sb, b)
                for n in range(2):
                    last = tp(ps[:, M0, n * HALF:(n + 1) * HALF], rec[0:HALF, b.r % 4, n, 0:D], ident[0:HALF, 0:HALF])
                last.then_inc(z3T_ps, 1)

            def logits(b):
                wait(pe, z3T_sb, b)
                wait(pe, h_sb, b.lag(-6))
                for n in range(2):
                    last = mm(ps[0:HALF, M1, n * D:(n + 1) * D], z3T[:, b.r % 2, n * HALF:(n + 1) * HALF], w_r_sb[:],
                              start=True, stop=True)
                last.then_inc(lg_ps, 1)

            def ranks(b):
                wait(pe, onehot_sb, b)
                wait(pe, cn_sb, b.lag(-1))
                wait(pe, slots_moved, b.lag(1))
                oh = onehot[0:HALF, b.r % 2]
                mm(ps[0:HALF, MID, 0:2 * E], before[0:HALF], oh.rearrange("p c e -> p (c e)"), start=True, stop=False,
                   skip_group_check=True)
                mm(ps[0:HALF, MID, E:2 * E], ones_bf[0:HALF], oh[:, 0, :], start=False, stop=True, skip_group_check=True)
                for n in range(2):
                    last = mm(ps[0:HALF, MID, 2 * E:3 * E], ones_bf[0:HALF], oh[:, n, :], start=False, stop=(n == 1),
                              skip_group_check=True)
                last.then_inc(rank_ps, 1)

            x_transpose(Row(0, 0))

            def step(i):
                j, n, s, b, u, r = i.lag(1), i.lag(2), i.lag(3), i.lag(4), i.lag(5), i.lag(6)
                for hd in range(HEADS):
                    if b.live():
                        scores_T(b, hd)
                    if n.live():
                        scores(n, hd)
                    if hd == 0 and i.live():
                        conv(i, 0)
                    if hd == 1:
                        if s.live():
                            max_transpose(s)
                        if i.live():
                            conv(i, 1)
                    if hd == 2 and j.live():
                        project_v(j)
                    if hd == 3:
                        if r.live():
                            z3_transpose(r)
                        if u.live():
                            heads_transpose(u)
                    if hd == 4:
                        if i.lag(-1).live():
                            x_transpose(i.lag(-1))
                        if r.live():
                            logits(r)
                    if hd == 5 and u.live():
                        c_transpose(u)
                    if hd < 2:
                        if u.live():
                            values(u, hd + 6)
                    elif b.live():
                        values(b, hd - 2)
                    if hd == 5 and i.live():
                        z_transpose(i)
                    if hd == 6:
                        if i.live():
                            project_qk(i)
                        if u.live():
                            project_out(u)
                    if hd == 7 and r.live():
                        ranks(r)

            pipeline(pe, step)
            pe.wait_ge(loads, 16 * 13)
            tp(ps[:, 0, 0:E], b_1_rows[:], ident[0:E, 0:E]).then_inc(b1T_ps, 1)
            pe.wait_ge(b1T_sb, 1)

            def step_b(t):
                if t.live(TILES):
                    wait_dma(pe, t_in, t, rows=TILES)
                    wait(pe, tT_sb, t.lag(2), rows=TILES)
                    tp(ps[:, 0 + t.r % 2, 0:128], tile_in[:, t.r % RING, 0:D], ident[:]).then_inc(tT_ps, 1)
                b = t.lag(1)
                if b.live(TILES):
                    c = b.r % 2
                    wait(pe, expert_sb, b, rows=TILES)
                    wait(pe, tT_sb, b, rows=TILES)
                    wait(pe, hid_sb, b.lag(2), rows=TILES)
                    mm(ps[:, 2 + c, 0:128], expert[:, b.r % 4, 0:D], tT[:, c, :], start=True, stop=True).then_inc(hid_ps, 1)
                b = t.lag(2)
                if b.live(TILES):
                    c = b.r % 2
                    wait(pe, hid_sb, b, rows=TILES)
                    wait(pe, y_half, b.lag(2), rows=TILES)
                    mm(ps[:, 6 + c, 0:D], hidT[:, c, :], expert[:, b.r % 4, D:2 * D], start=True, stop=True).then_inc(y_ps, 1)

            pipeline_b(pe, step_b, upto=2)


_INS = ["x", "L0_tok_W", "L0_tok_b", "L0_attn_w_qkv", "L0_attn_w_out", "L0_attn_b_out", "L0_attn_gamma", "L0_attn_beta",
        "L0_ffn_Wr", "L0_ffn_br", "L0_ffn_W1", "L0_ffn_b1", "L0_ffn_W2", "L0_ffn_b2"]


def kernel(**inputs):
    import numpy as _np
    import concourse.bacc as _bacc
    from concourse import mybir as _mybir
    from concourse.bass_utils import run_bass_kernel_spmd as _run

    nc = _bacc.Bacc("TRN2", target_bir_lowering=False, num_devices=1)
    arrays, args = {}, []
    for name in _INS:
        a = _np.ascontiguousarray(inputs[name])
        arrays[f"in_{name}_dram"] = a
        args.append(nc.dram_tensor(f"in_{name}_dram", a.shape, _mybir.dt.from_np(a.dtype), kind="ExternalInput").ap())
    b, t, d = inputs["x"].shape
    taps = inputs["L0_tok_W"].shape[0] // d
    shape = (b, t - taps + 1, d)
    args.append(nc.dram_tensor("out_0_dram", shape, _mybir.dt.float32, kind="ExternalOutput").ap())
    build(nc, *args)
    r = _run(nc, [arrays], core_ids=[0])
    return r.results[0]["out_0_dram"]
```

```python
from contextlib import ExitStack

import concourse.bass as bass
from concourse import mybir

F32 = mybir.dt.float32
BF16 = mybir.dt.bfloat16
I32 = mybir.dt.int32
ALU = mybir.AluOpType
ACT = mybir.ActivationFunctionType
AX = mybir.AxisListType

EPS = 1e-5
HEADS = 8
NEG = -1e30
UNROLL = 4


def build(nc, x, tok_w, tok_b, w_qkv, w_out, b_out, gamma, beta, w_r, b_r, w_1, b_1, w_2, b_2, out):
    NB, TIN, D = x.shape
    TAPS = tok_w.shape[0] // D
    T = TIN - TAPS + 1
    HALF = T // 2
    HD = D // HEADS
    E = w_r.shape[1]
    TOKENS = NB * T
    TRI = 3 * HALF
    REC = 2 * D + 2
    GATE, IDCOL = 2 * D, 2 * D + 1
    BIN = 64 * 128
    TILES = TOKENS // 128 + E - 1
    PAD_TILE = E * BIN // 128
    NO_TOKEN = 1 << 20
    PARTS = 3
    ROWS = 6 * HD
    STACKS = [(0, 0, 1, 1), (1, 0, 3, 0), (0, 2 * HD, 1, 1), (1, 2 * HD, 4, 0), (0, 4 * HD, 0, 2), (1, 4 * HD, 3, 2)]
    MROWS = ROWS + PARTS
    LAST = 7
    assert TOKENS % 128 == 0 and T % 2 == 0 and TOKENS + 128 <= BIN and D == 128 and E == 8

    bins = nc.dram_tensor("bins", [E * BIN + 128, REC], F32, kind="Internal").ap()
    splits = nc.dram_tensor("splits", [2, 2 * PARTS, 128, T], BF16, kind="Internal").ap()

    with ExitStack() as ctx:
        def sb(name, shape, dt=F32):
            return ctx.enter_context(nc.sbuf_tensor(name, shape, dt))

        def sem(name):
            return ctx.enter_context(nc.semaphore(name))

        tok_w_sb = sb("tok_w_sb", [128, TAPS, D])
        w_qkv_sb = sb("w_qkv_sb", [128, 3 * D])
        w_out_sb = sb("w_out_sb", [128, D])
        gamma_sb = sb("gamma_sb", [128, 1])
        beta_sb = sb("beta_sb", [128, 1])
        tok_b_sb = sb("tok_b_sb", [128, D])
        b_out_sb = sb("b_out_sb", [1, D])
        w_r_sb = sb("w_r_sb", [128, D])
        b_r_sb = sb("b_r_sb", [128, E])
        lg = sb("lg", [128, 2, E])
        W_COLS = 3 * D + 1
        experts = sb("experts", [128, E, W_COLS])
        w_raw = sb("w_raw", [128, 2, D])
        w_q = sb("w_q", [128, D])
        w_k = sb("w_k", [128, D])
        w_v = sb("w_v", [128, D])
        gamma_q = sb("gamma_q", [128, 1])
        qk_bias = sb("qk_bias", [128, 2])
        v_bias = sb("v_bias", [128, 1])
        o_bias_row = sb("o_bias_row", [1, D])
        o_bias = sb("o_bias", [128, 2, D])
        ident = sb("ident", [128, 128])
        ident_bf = sb("ident_bf", [128, 128], BF16)
        causal = sb("causal", [128, 2, HALF], BF16)
        before = sb("before", [128, HALF], BF16)
        ones_bf = sb("ones_bf", [128, HALF], BF16)
        one_col = sb("one_col", [128, 1])
        ones_row = sb("ones_row", [1, 128])
        neg_half = sb("neg_half", [128, 4])
        iota_b = sb("iota_b", [128, E], I32)
        iota_i = sb("iota_i", [128, 2 * E], I32)
        bin_start = sb("bin_start", [128, E])
        rank_weight = sb("rank_weight", [128, E])
        token_i = sb("token_i", [128, 2], I32)
        token = sb("token", [128, 2])
        next_slot = sb("next_slot", [128, E])
        blank = sb("blank", [128, REC])

        xt = sb("xt", [128, 4, 2, D])
        xT = sb("xT", [128, 2, TIN])
        h = sb("h", [128, 2, 2, D])
        stats = sb("stats", [128, 2, 6])
        mv = sb("mv", [128, 2, 2, 2])
        var_e = sb("var_e", [128, 4])
        rstd = sb("rstd", [128, 2, 4])
        one_r = sb("one_r", [128, 2])
        neg_m = sb("neg_m", [128, 2])
        neg_mr = sb("neg_mr", [128, 2])
        base_h = sb("base_h", [128, 2, D])
        base = sb("base", [128, NB, 2, D])
        z = sb("z", [128, 2, 2, D])
        zT = sb("zT", [128, 2, T])
        qk = sb("qk", [128, 2, 2, T])
        rest = sb("rest", [128, 2, 2, T])
        parts = sb("parts", [128, 2, 2 * PARTS, T], BF16)
        Q = sb("Q", [128, 4, HEADS, T], BF16)
        K = sb("K", [128, 4, HEADS, T], BF16)
        V = sb("V", [128, 4, 2, HEADS, 32])
        nmax3 = sb("nmax3", [128, 2, HEADS, 3])
        nmax = sb("nmax", [128, 2, HEADS])
        nmax_rest = sb("nmax_rest", [128, 2, HEADS])
        nmax_parts = sb("nmax_parts", [128, 2, 2, PARTS, HEADS], BF16)
        nmaxT = sb("nmaxT", [PARTS * HEADS, 2, T], BF16)
        P = sb("P", [128, HEADS, TRI])
        oT = sb("oT", [128, 2, T])
        rsum = sb("rsum", [128, 16])
        cn = sb("cn", [128, 2, 2, D])
        cT = sb("cT", [128, 2, T])
        rec = sb("rec", [128, 4, 2, REC])
        stats2 = sb("stats2", [128, 2, 6])
        mv2 = sb("mv2", [128, 2, 2, 2])
        var2_e = sb("var2_e", [128, 2])
        rstd2 = sb("rstd2", [128, 2, 2])
        neg_m2 = sb("neg_m2", [128, 2])
        neg_mz2 = sb("neg_mz2", [128, 2, 2])
        z3T = sb("z3T", [128, 2, T])
        lmax = sb("lmax", [128, 2])
        ldiff = sb("ldiff", [128, 2, 2, E])
        lexp = sb("lexp", [128, 2, 2, E])
        lsum = sb("lsum", [128, 2])
        hit = sb("hit", [128, 2, E])
        first = sb("first", [128, 2])
        onehot = sb("onehot", [128, 2, 2, E], BF16)
        pos = sb("pos", [128, 2, E])
        pos_own = sb("pos_own", [128, 2, E])
        slot_f = sb("slot_f", [128, 2])
        slot = sb("slot", [128, 4, 2], I32)

        RING, Y_RING, GROUP = 16, 8, 4
        tile_in = sb("tile_in", [128, RING, REC])
        tT = sb("tT", [128, 2, 128])
        b_1_rows = sb("b_1_rows", [E, D])
        expert = sb("expert", [128, 4, W_COLS])
        hidT = sb("hidT", [128, 2, 128])
        y_part = sb("y_part", [128, 2, D])
        y = sb("y", [128, Y_RING, D])
        count_i = sb("count_i", [1, E], I32)
        tiles_i = sb("tiles_i", [1, E], I32)
        tiles_f = sb("tiles_f", [1, E])
        skip = sb("skip", [1, E])
        tiles_end = sb("tiles_end", [1, E])
        one_e = sb("one_e", [1, E])
        tile_no_i = sb("tile_no_i", [1, TILES], I32)
        tile_no = sb("tile_no", [1, TILES])
        passed = sb("passed", [1, TILES, E])
        skipped = sb("skipped", [1, TILES, E])
        expert_f = sb("expert_f", [1, TILES])
        start_f = sb("start_f", [1, TILES])
        row_f = sb("row_f", [1, TILES])
        row_i = sb("row_i", [1, TILES], I32)
        expert_i = sb("expert_i", [1, TILES], I32)
        tail_i = sb("tail_i", [1, E], I32)

        ps = ctx.enter_context(nc.psum_tensor("ps", [128, 8, 512], F32))
        NAT, TRN, AV, MID, M0, M1 = 0, 2, 4, 5, 6, 7

        loads, tokeniser_in = sem("loads"), sem("tokeniser_in")
        s_ident, s_fill = sem("s_ident"), sem("s_fill")
        s_const = sem("s_const")
        s_chain = sem("s_chain")
        s_setup_pe = sem("s_setup_pe")
        s_setup = sem("s_setup")
        x_in = [sem(f"x_in{n}") for n in range(4)]
        xT_ps, xT_sb = sem("xT_ps"), sem("xT_sb")
        conv_ps, h_sb, st1, mv_sb = sem("conv_ps"), sem("h_sb"), sem("st1"), sem("mv_sb")
        pool_var, pool_rstd, pool_sc, base_part, base_sb = (sem(n) for n in ("pool_var", "pool_rstd", "pool_sc", "base_part", "base_sb"))
        z_sb, zT_ps, zT_sb = sem("z_sb"), sem("zT_ps"), sem("zT_sb")
        qk_ps, qk_sb, v_ps, v_sb = sem("qk_ps"), sem("qk_sb"), sem("v_ps"), sem("v_sb")
        part1, rest1, part2, part3 = sem("part1"), sem("rest1"), sem("part2"), sem("part3")
        split_out = [sem(f"split_out{n}") for n in range(2)]
        third_out = [sem(f"third_out{n}") for n in range(2)]
        stack_in = [sem(f"stack_in{n}") for n in range(2)]
        nat_ps, max_sb = sem("nat_ps"), sem("max_sb")
        nm_sb, nmp1, nmr1, nmp2, nmp3 = (sem(n) for n in ("nm_sb", "nmp1", "nmr1", "nmp2", "nmp3"))
        nmT_ps, nmT_sb = sem("nmT_ps"), sem("nmT_sb")
        max_in = [sem(f"max_in{n}") for n in range(2)]
        trn_ps, exp_sb, sel_sb, av_ps = sem("trn_ps"), sem("exp_sb"), sem("sel_sb"), sem("av_ps")
        oT_sb, o_ps, rsum_sb, cn_sb = sem("oT_sb"), sem("o_ps"), sem("rsum_sb"), sem("cn_sb")
        cT_ps, cT_sb, proj_ps, h2_sb = sem("cT_ps"), sem("cT_sb"), sem("proj_ps"), sem("h2_sb")
        st2, mv2_sb, pool_var2, rstd2_sb, z3_sb = (sem(n) for n in ("st2", "mv2_sb", "pool_var2", "rstd2_sb", "z3_sb"))
        z3T_ps, z3T_sb, lg_ps, lg_sb = (sem(n) for n in ("z3T_ps", "z3T_sb", "lg_ps", "lg_sb"))
        lmax_sb, ldiff_sb, lexp_sb, lsum_sb, gate_sb = (sem(n) for n in ("lmax_sb", "ldiff_sb", "lexp_sb", "lsum_sb", "gate_sb"))
        hit_sb, first_sb, onehot_sb = sem("hit_sb"), sem("first_sb"), sem("onehot_sb")
        rank_ps, pos_sb, slots_moved, own_sb, slotf_sb, slot_sb = (sem(n) for n in ("rank_ps", "pos_sb", "slots_moved", "own_sb", "slotf_sb", "slot_sb"))
        id_sb, token_moved = sem("id_sb"), sem("token_moved")
        scattered = [sem(f"scattered{n}") for n in range(4)]
        pool_rstd2 = sem("pool_rstd2")
        s_plan = sem("s_plan")
        s_tail = sem("s_tail")
        b1T_ps, b1T_sb, expert_sb, y_half = sem("b1T_ps"), sem("b1T_sb"), sem("expert_sb"), sem("y_half")
        passed_waits = sem("passed_waits")
        s_plan2 = sem("s_plan2")
        s_ptail = sem("s_ptail")
        pad_in = sem("pad_in")
        tail_in = sem("tail_in")
        t_in = [sem(f"t_in{n}") for n in range(RING)]
        tT_ps, tT_sb, hid_ps, hid_sb, y_ps, y_sb = (
            sem(n) for n in ("tT_ps", "tT_sb", "hid_ps", "hid_sb", "y_ps", "y_sb"))
        y_out = [sem(f"y_out{n}") for n in range(Y_RING)]

        class Row:

            def __init__(self, k, r, unroll=UNROLL):
                self.k, self.r, self.unroll = k, r, unroll
                self.n = unroll * k + r
                self.ap = bass.ds(self.n, 1)

            def lag(self, d):
                return Row(self.k, self.r - d, self.unroll)

            def live(self, rows=NB):
                return not isinstance(self.k, int) or 0 <= self.n < rows

        def wait_apart(eng):
            eng.sem_inc(passed_waits, 1)

        def wait(eng, s, b, per=1, upto=None, rows=NB):
            upto = per if upto is None else upto
            if isinstance(b.k, int):
                n, upto = (b.n, upto) if b.n < rows else (rows - 1, per)
                if per * n + upto > 0:
                    eng.wait_ge(s, per * n + upto)
            else:
                eng.wait_ge(s, b.k * (per * b.unroll) + (per * b.r + upto))
                if eng is nc.sync:
                    wait_apart(eng)

        def wait_dma(eng, ring, b, dmas=1, rows=NB):
            m = len(ring)
            if isinstance(b.k, int):
                if b.n >= 0:
                    eng.wait_ge(ring[b.n % m], 16 * dmas * (b.n // m + 1))
            else:
                eng.wait_ge(ring[b.r % m], b.k * (16 * dmas * b.unroll // m) + 16 * dmas * (b.r // m + 1))
                if eng is nc.sync:
                    wait_apart(eng)

        def split(c, n):
            return parts[:, c, 2 - n:4 + n:1 + 2 * n, :]

        def bass_diag(a):
            return bass.AP(a.tensor, a.offset, [list(a.ap[0]), [T, 2], [1, HALF]])

        def pipeline(eng, step):
            start = LAST + 3
            loops = (NB - 2 - start) // UNROLL
            for i in range(start):
                step(Row(0, i))
            with eng.Fori(1, 1 + loops) as k:
                for j in range(UNROLL):
                    step(Row(k, start - UNROLL + j))
            for i in range(start + loops * UNROLL, NB + LAST):
                step(Row(0, i))

        def load_values(eng, table, first, count, max_val):
            return nc.values_load_multi_w_load_instructions(table[0:1, bass.ds(first, count)], engines=[eng.engine],
                                                            min_val=0, max_val=max_val)[1]

        def pipeline_b(eng, step, upto, lag=0, table=None, max_val=0):
            start = RING
            loops = (TILES - start) // RING
            rest = start + loops * RING

            def steps(k, first, at, count):
                values = []
                for j in range(count):
                    t = Row(k, first + j - lag, RING)
                    if table is not None and j % GROUP == 0 and (first + j < TILES or not isinstance(k, int)):
                        values += load_values(eng, table, at + j, min(GROUP, TILES - first - j) if isinstance(k, int) else GROUP,
                                              max_val)
                    if t.live(TILES + upto):
                        step(t, *values[j:j + 1])

            steps(0, 0, 0, start)
            with eng.Fori(0, loops) as k:
                steps(k, start, k * RING + start, RING)
            steps(0, rest, rest, TILES + upto - rest)

        def fill_tails(eng, first):
            eng.wait_ge(s_tail, 1)
            for e in range(first, E, 2):
                end = eng.value_load(tail_i[0:1, e:e + 1], min_val=e * BIN, max_val=e * BIN + TOKENS)
                eng.dma_start(bins[bass.ds(end, 128), :], blank[:]).then_inc(tail_in, 16)

        block = ctx.enter_context(nc.Block())

        @block.sync
        def _(sp):
            def load_x(b):
                wait(sp, xT_ps, b.lag(4))
                sp.dma_start(xt[:, b.r % 4, :, :], x[b.n].rearrange("(c p) f -> p c f", p=128)).then_inc(x_in[b.r % 4], 16)

            load_x(Row(0, 0))
            sp.dma_start(tok_w_sb[:], tok_w.rearrange("(k f) u -> f k u", k=TAPS)).then_inc(tokeniser_in, 16)
            sp.dma_start(tok_b_sb[:], tok_b.rearrange("(a u) -> a u", a=1).partition_broadcast(128)).then_inc(tokeniser_in, 16)
            load_x(Row(0, 1))
            for dst, src in (
                (w_qkv_sb[:], w_qkv),
                (gamma_sb[:], gamma.rearrange("(p a) -> p a", a=1)),
                (beta_sb[:], beta.rearrange("(p a) -> p a", a=1)),
                (w_out_sb[:], w_out),
                (b_out_sb[:], b_out.rearrange("(a u) -> a u", a=1)),
                (w_r_sb[:, 0:E], w_r),
                (b_r_sb[:], b_r.rearrange("(a u) -> a u", a=1).partition_broadcast(128)),
            ):
                sp.dma_start(dst, src).then_inc(loads, 16)

            later_loads = [
                (experts[:, :, 0:D], w_1.rearrange("e h f -> h e f")),
                (experts[:, :, D:2 * D], w_2.rearrange("e h f -> h e f")),
                (b_1_rows[:], b_1),
                (experts[:, :, 2 * D:3 * D], b_2.rearrange("(a e) f -> a e f", a=1).partition_broadcast(128)),
            ]

            def step(i):
                b = i.lag(-2)
                if b.live():
                    load_x(b)
                b = i.lag(1)
                if b.live():
                    d = b.r % 2
                    wait_dma(sp, stack_in, b.lag(2), dmas=len(STACKS))
                    for n, part, out_sem in ((0, part1, split_out), (1, part2, split_out), (2, part3, third_out)):
                        wait(sp, part, b)
                        sp.dma_start(splits[d, 2 - n:4 + n:1 + 2 * n].rearrange("s p t -> p s t"),
                                     split(d, n)).then_inc(out_sem[d], 16)
                b = i.lag(3)
                if b.live():
                    wait(sp, nmT_sb, b)
                    wait(sp, trn_ps, b.lag(4), per=HEADS)
                    sp.dma_start(Q[ROWS:MROWS, b.r % 4], nmaxT[:, b.r % 2, :]).then_inc(max_in[b.r % 2], 16)
                b = i.lag(1)
                if b.live():
                    d, c = b.r % 2, b.r % 4
                    wait(sp, trn_ps, b.lag(4), per=HEADS)
                    for n, (operand, first_row, where, other) in enumerate(STACKS):
                        if n == 0:
                            wait_dma(sp, split_out, b, dmas=2)
                        if n == 4:
                            wait_dma(sp, third_out, b)
                        rows = bass.AP(splits.tensor, splits[d, where].offset,
                                       [[HEADS * T, HD], [other * 128 * T, 2], [1, HEADS * T]])
                        sp.dma_start((Q, K)[operand][first_row:first_row + 2 * HD, c].rearrange("p h t -> p (h t)"),
                                     rows).then_inc(stack_in[d], 16)
                if isinstance(i.k, int) and 0 <= i.n - 5 < len(later_loads):
                    dst, src = later_loads[i.n - 5]
                    sp.dma_start(dst, src).then_inc(loads, 16)
                if isinstance(i.k, int) and i.n == 4:
                    sp.dma_start(bins[E * BIN:E * BIN + 128, :], blank[:]).then_inc(pad_in, 16)

            pipeline(sp, step)

            fill_tails(sp, 0)
            sp.wait_ge(s_plan, 1)

            def step_b(t, row):
                if isinstance(t.k, int) and t.n == 0:
                    for n in range(4):
                        sp.wait_ge(scattered[n], 16 * 2 * NB // 4)
                    sp.wait_ge(tail_in, 16 * E)
                    sp.wait_ge(pad_in, 16)
                b = t.lag(RING)
                if not (isinstance(b.k, int) and b.n < 0):
                    wait_dma(sp, y_out, b, rows=TILES)
                sp.dma_start(tile_in[:, t.r % RING, :], bins[bass.ds(row * 128, 128), :]).then_inc(t_in[t.r % RING], 16)

            pipeline_b(sp, step_b, upto=0, table=row_i, max_val=PAD_TILE)
            for n in range(Y_RING):
                sp.wait_ge(y_out[n], 16 * len(range(n, TILES, Y_RING)))

        @block.gpsimd
        def _(pool):
            g = nc.gpsimd
            chain = [0]

            def link(ins):
                chain[0] += 1
                ins.then_inc(s_chain, 1)
                pool.wait_ge(s_chain, chain[0])

            link(g.memset(ident[:], 1.0))
            link(g.affine_select(out=ident[:], in_=ident[:], compare_op=ALU.is_equal, fill=0.0, base=0,
                                 pattern=[[-1, 128]], channel_multiplier=1))
            g.tensor_copy(ident_bf[:], ident[:]).then_inc(s_ident, 1)
            g.memset(causal[:], 0.0)
            g.memset(ones_bf[:], 1.0)
            g.memset(neg_half[:], -0.5)
            g.memset(one_e[:], 1.0)
            link(g.memset(before[:], 1.0))
            link(g.affine_select(out=causal[:], in_=causal[:], compare_op=ALU.is_ge, fill=NEG, base=0,
                            pattern=[[0, 2], [-1, HALF]], channel_multiplier=1))
            link(g.affine_select(out=before[:], in_=before[:], compare_op=ALU.is_gt, fill=0.0, base=0,
                            pattern=[[1, HALF]], channel_multiplier=-1))
            link(g.iota(iota_i[:, 0:E], [[BIN, E]], base=0, channel_multiplier=0))
            link(g.iota(iota_i[:, E:2 * E], [[-1, E]], base=E, channel_multiplier=0))
            link(g.iota(token_i[:], [[HALF, 2]], base=0, channel_multiplier=1))
            link(g.iota(tile_no_i[:], [[1, TILES]], base=0, channel_multiplier=0))
            link(g.iota(iota_b[:], [[BIN, E]], base=-127, channel_multiplier=0))
            link(g.tensor_copy(bin_start[:], iota_b[:]))
            link(g.tensor_copy(next_slot[:], iota_i[:, 0:E]))
            link(g.tensor_copy(rank_weight[:], iota_i[:, E:2 * E]))
            link(g.tensor_copy(token[:], token_i[:]))
            g.tensor_copy(tile_no[:], tile_no_i[:]).then_inc(s_const, 1)
            pool.wait_ge(s_const, 1)

            def keep_causal(b, hd):
                wait(pool, exp_sb, b, per=HEADS, upto=hd + 1)
                wait_apart(pool)
                v = P[0:HALF, hd, :]
                diag = bass_diag(v)
                g.affine_select(out=diag, in_=diag, compare_op=ALU.is_ge, fill=0.0, base=0,
                                pattern=[[0, 2], [1, HALF]], channel_multiplier=-1).then_inc(sel_sb, 1)

            def norm_factors(b):
                c = b.r % 2
                wait(pool, mv_sb, b)
                wait(pool, z_sb, b.lag(2), per=2)
                wait(pool, base_part, b.lag(1), per=2)
                wait_apart(pool)
                g.tensor_scalar(var_e[0:HALF, 0:2], mv[0:HALF, c, :, 1], 1.0, EPS, ALU.mult, ALU.add)
                g.tensor_scalar(neg_m[0:HALF], mv[0:HALF, c, :, 0], -1.0, 0.0, ALU.mult, ALU.add)
                g.tensor_scalar(var_e[0:HALF, 2:4], mv[0:HALF, c, :, 1], 1.0 + EPS, EPS * EPS, ALU.mult,
                                ALU.add).then_inc(pool_var, 1)
                wait(pool, pool_var, b)
                g.tensor_tensor(rstd[0:HALF, c, :], var_e[0:HALF], neg_half[0:HALF], ALU.pow).then_inc(pool_rstd, 1)
                wait(pool, pool_rstd, b)
                g.tensor_tensor(neg_mr[0:HALF], neg_m[0:HALF], rstd[0:HALF, c, 0:2], ALU.mult)
                g.tensor_scalar(one_r[0:HALF], rstd[0:HALF, c, 0:2], 1.0, 1.0, ALU.mult, ALU.add).then_inc(pool_sc, 1)

            def add_bias(b):
                wait(pool, base_part, b, per=2)
                if isinstance(b.k, int) and b.n == 0:
                    pool.wait_ge(s_setup, 1)
                g.tensor_tensor(base[0:HALF, b.ap, :, :].rearrange("p a c u -> p (a c u)"),
                                base_h[0:HALF].rearrange("p c u -> p (c u)"),
                                o_bias[0:HALF].rearrange("p c u -> p (c u)"), ALU.add).then_inc(base_sb, 1)

            def norm_factor2(b):
                c = b.r % 2
                wait(pool, mv2_sb, b)
                wait(pool, z3_sb, b.lag(2), per=2)
                wait_apart(pool)
                g.tensor_scalar(neg_m2[0:HALF], mv2[0:HALF, c, :, 0], -1.0, 0.0, ALU.mult, ALU.add)
                g.tensor_scalar(var2_e[0:HALF], mv2[0:HALF, c, :, 1], 1.0, EPS, ALU.mult, ALU.add).then_inc(pool_var2, 1)
                wait(pool, pool_var2, b)
                g.tensor_tensor(rstd2[0:HALF, c, :], var2_e[0:HALF], neg_half[0:HALF, 0:2], ALU.pow).then_inc(pool_rstd2, 1)
                wait(pool, pool_rstd2, b)
                g.tensor_tensor(neg_mz2[0:HALF, c], neg_m2[0:HALF], rstd2[0:HALF, c], ALU.mult).then_inc(rstd2_sb, 1)

            def scatter(b, n):
                c = b.r % 4
                if n == 0:
                    wait(pool, slot_sb, b)
                    wait(pool, gate_sb, b)
                    wait(pool, id_sb, b)
                    wait(pool, z3_sb, b, per=2)
                    wait_apart(pool)
                g.indirect_dma_start(bins, bass.IndirectOffsetOnAxis(ap=slot[0:HALF, c, n:n + 1], axis=0),
                                     rec[0:HALF, c, n, :], None, bounds_check=E * BIN - 1,
                                     oob_is_err=False).then_inc(scattered[b.r % 4], 16)

            def step(i):
                b, r, q = i.lag(4), i.lag(6), i.lag(7)
                for hd in range(HEADS):
                    if b.live():
                        keep_causal(b, hd)
                    if hd == 0 and r.live():
                        norm_factor2(r)
                    if hd == 2 and q.live():
                        scatter(q, 0)
                    if hd == 3 and i.live():
                        norm_factors(i)
                    if hd == 5 and q.live():
                        scatter(q, 1)
                    if hd == 7 and i.live():
                        add_bias(i)

            pipeline(pool, step)

            def step_b(t):
                c = t.r % Y_RING
                wait(pool, y_sb, t, rows=TILES)
                wait_apart(pool)
                g.indirect_dma_start(out.rearrange("b t u -> (b t) u"),
                                     bass.IndirectOffsetOnAxis(ap=tile_in[:, t.r % RING, IDCOL:REC].bitcast(I32), axis=0),
                                     y[:, c, :], None, bounds_check=TOKENS - 1,
                                     oob_is_err=False).then_inc(y_out[c], 16)

            pipeline_b(pool, step_b, upto=3, lag=3)

        @block.scalar
        def _(act):
            a = nc.scalar

            def exp_scores(b, hd):
                wait(act, trn_ps, b, per=HEADS, upto=hd + 1)
                wait(act, av_ps, b.lag(1), per=HEADS, upto=hd + 1)
                a.activation(P[0:HALF, hd, :], ps[0:HALF, TRN + hd % 2, 0:TRI], ACT.Exp).then_inc(exp_sb, 1)

            def xT_copy(b):
                wait(act, xT_ps, b)
                wait(act, conv_ps, b.lag(2))
                a.copy(xT[:, b.r % 2, :], ps[:, M0, 0:TIN]).then_inc(xT_sb, 1)

            def zT_copy(b):
                wait(act, zT_ps, b)
                wait(act, v_ps, b.lag(2))
                a.copy(zT[:, b.r % 2, :], ps[:, M1, 0:T]).then_inc(zT_sb, 1)

            def qk_copy(b):
                c = b.r % 2
                if isinstance(b.k, int) and b.n == 0:
                    act.wait_ge(s_setup, 1)
                wait(act, qk_ps, b)
                wait(act, rest1, b.lag(2))
                for n in range(2):
                    a.activation(qk[:, c, n, :], ps[:, MID, n * T:(n + 1) * T], ACT.Identity,
                                 bias=qk_bias[:, n:n + 1]).then_inc(qk_sb, 1)
                wait(act, qk_sb, b, per=2)
                wait_dma(act, split_out, b.lag(2), dmas=2)
                a.copy(split(c, 0), qk[:, c]).then_inc(part1, 1)

            def second_parts(b):
                wait(act, rest1, b)
                a.copy(split(b.r % 2, 1), rest[:, b.r % 2]).then_inc(part2, 1)

            def v_copy(b):
                wait(act, v_ps, b)
                wait(act, av_ps, b.lag(4), per=HEADS)
                a.copy(V[0:HALF, b.r % 4, :, :, 0:HD].rearrange("p c h d -> p (c h) d"),
                       ps[0:HALF, M0, 0:2 * D].rearrange("p (c d) -> p c d", d=HD)).then_inc(v_sb, 1)

            def nmaxT_copy(b):
                wait(act, nmT_ps, b)
                wait_dma(act, max_in, b.lag(2))
                a.copy(nmaxT[:, b.r % 2, :], ps[0:PARTS * HEADS, MID, 0:T // 2 + 0].bitcast(BF16)[:, 0:T]).then_inc(nmT_sb, 1)

            def oT_copy(b):
                wait(act, av_ps, b, per=HEADS)
                wait(act, o_ps, b.lag(1))
                a.copy(oT[:], ps[:, AV, 0:2 * T].rearrange("p (c t) -> p c t", c=2)).then_inc(oT_sb, 1)

            def cT_copy(b):
                wait(act, cT_ps, b)
                wait(act, proj_ps, b.lag(2))
                a.copy(cT[:, b.r % 2, :], ps[:, M0, 0:T]).then_inc(cT_sb, 1)

            def z3T_copy(b):
                wait(act, z3T_ps, b)
                wait(act, lg_ps, b.lag(2))
                a.copy(z3T[:, b.r % 2, :], ps[:, M0, 0:T]).then_inc(z3T_sb, 1)

            def residual(b):
                c = b.r % 2
                wait(act, pool_sc, b)
                wait(act, base_sb, b.lag(1))
                for n in range(2):
                    a.activation(base_h[0:HALF, n], h[0:HALF, c, n], ACT.Identity, bias=neg_mr[0:HALF, n:n + 1],
                                 scale=one_r[0:HALF, n:n + 1]).then_inc(base_part, 1)

            def normalise2(b):
                c = b.r % 2
                wait(act, rstd2_sb, b)
                for n in range(2):
                    a.activation(rec[0:HALF, b.r % 4, n, 0:D], rec[0:HALF, b.r % 4, n, D:2 * D], ACT.Identity,
                                 bias=neg_mz2[0:HALF, c, n:n + 1], scale=rstd2[0:HALF, c, n:n + 1]).then_inc(z3_sb, 1)

            def logit_exp(b):
                wait(act, ldiff_sb, b)
                wait(act, lsum_sb, b.lag(2))
                a.activation(lexp[0:HALF, b.r % 2], ldiff[0:HALF, b.r % 2], ACT.Exp).then_inc(lexp_sb, 1)

            act.wait_ge(s_ident, 1)
            a.copy(one_col[:], ident[:, 0:1])
            xT_copy(Row(0, 0))

            def step(i):
                s, b, u, r = i.lag(3), i.lag(4), i.lag(5), i.lag(6)
                for hd in range(HEADS):
                    if hd == 2:
                        if s.live():
                            nmaxT_copy(s)
                        if u.live():
                            oT_copy(u)
                    if hd == 3 and i.lag(1).live():
                        v_copy(i.lag(1))
                    if hd == 4 and r.live():
                        z3T_copy(r)
                    if hd == 5 and i.lag(-1).live():
                        xT_copy(i.lag(-1))
                    if hd == 6 and u.live():
                        cT_copy(u)
                    if hd == 7 and i.live():
                        qk_copy(i)
                    if b.live():
                        exp_scores(b, hd)
                    if hd == 0 and i.lag(1).live():
                        second_parts(i.lag(1))
                    if hd == 2 and r.live():
                        normalise2(r)
                    if hd == 6:
                        if i.live():
                            zT_copy(i)
                        if r.live():
                            logit_exp(r)
                        if i.live():
                            residual(i)

            pipeline(act, step)

            fill_tails(act, 1)
            act.wait_ge(b1T_sb, 1)

            def step_b(t):
                if t.live(TILES):
                    wait(act, tT_ps, t, rows=TILES)
                    wait(act, hid_ps, t.lag(2), rows=TILES)
                    a.copy(tT[:, t.r % 2, :], ps[:, 0 + t.r % 2, 0:128]).then_inc(tT_sb, 1)
                b = t.lag(1)
                if b.live(TILES):
                    wait(act, hid_ps, b, rows=TILES)
                    wait(act, y_ps, b.lag(2), rows=TILES)
                    a.activation(hidT[:, b.r % 2, :], ps[:, 2 + b.r % 2, 0:128], ACT.Relu,
                                 bias=expert[:, b.r % 4, 3 * D:W_COLS]).then_inc(hid_sb, 1)

            pipeline_b(act, step_b, upto=1)

        @block.vector
        def _(dve):
            v = nc.vector
            v.memset(ones_row[:], 1.0).then_inc(s_fill, 1)
            v.memset(V[:], 0.0).then_inc(s_fill, 1)
            v.memset(w_r_sb[:, E:D], 0.0).then_inc(s_fill, 1)
            v.memset(blank[:, 0:IDCOL], 0.0).then_inc(s_fill, 1)
            v.memset(blank[:, IDCOL:REC].bitcast(I32), NO_TOKEN).then_inc(s_fill, 1)
            dve.wait_ge(s_fill, 5)
            v.memset(V[:, :, :, :, HD:HD + 1], 1.0).then_inc(s_fill, 1)
            dve.wait_ge(loads, 16 * 7)
            for n in range(2):
                v.tensor_copy(w_raw[:, n, :].rearrange("p (d h) -> p d h", h=HEADS),
                              w_qkv_sb[:, n * D:(n + 1) * D].rearrange("p (h d) -> p d h", h=HEADS)).then_inc(s_setup_pe, 1)
            scale = float(HD) ** -0.5
            v.tensor_scalar(gamma_q[:], gamma_sb[:], scale, None, ALU.mult).then_inc(s_setup_pe, 1)
            dve.wait_ge(s_setup_pe, 3)
            v.tensor_scalar(w_q[:], w_raw[:, 0, :], gamma_q[:, 0:1], None, ALU.mult)
            v.tensor_scalar(w_k[:], w_raw[:, 1, :], gamma_sb[:, 0:1], None, ALU.mult)
            v.tensor_scalar(w_v[:], w_qkv_sb[:, 2 * D:3 * D], gamma_sb[:, 0:1], None, ALU.mult)
            dve.wait_ge(tokeniser_in, 32)

            def fold_biases():
                dve.wait_ge(s_ptail, 1)
                v.tensor_scalar(qk_bias[:, 0:1], ps[:, 4, 0:1], scale, None, ALU.mult)
                v.tensor_copy(qk_bias[:, 1:2], ps[:, 4, 1:2])
                v.tensor_copy(v_bias[:], ps[:, 4, 2:3]).then_inc(s_setup_pe, 1)
                dve.wait_ge(s_ptail, 2)
                v.tensor_tensor(o_bias_row[:], ps[0:1, 5, 0:D], b_out_sb[:], ALU.add).then_inc(s_setup_pe, 1)
                dve.wait_ge(s_ptail, 3)
                v.tensor_copy(o_bias[:, 0, :], ps[:, 4, 0:D])
                v.tensor_copy(o_bias[:, 1, :], ps[:, 4, 0:D]).then_inc(s_setup, 1)
                dve.wait_ge(s_const, 1)

            def row_max(b, hd):
                wait(dve, nat_ps, b, per=HEADS, upto=hd + 1)
                v.tensor_reduce(nmax3[0:HALF, b.r % 2, hd, :],
                                ps[0:HALF, NAT + hd % 2, 0:TRI].rearrange("p (c s) -> p c s", c=3),
                                AX.X, ALU.max, negate=True).then_inc(max_sb, 1)

            def negate_max(b):
                c = b.r % 2
                wait(dve, max_sb, b, per=HEADS)
                v.tensor_copy(nmax[0:HALF, 0, :], nmax3[0:HALF, c, :, 0])
                v.tensor_tensor(nmax[0:HALF, 1, :], nmax3[0:HALF, c, :, 1], nmax3[0:HALF, c, :, 2], ALU.min).then_inc(nm_sb, 1)

            def max_part0(b):
                wait(dve, nm_sb, b)
                wait(dve, nmT_ps, b.lag(2))
                v.tensor_copy(nmax_parts[0:HALF, b.r % 2, :, 0, :], nmax[0:HALF]).then_inc(nmp1, 1)

            def max_rest(b):
                wait(dve, nmp1, b)
                v.tensor_tensor(nmax_rest[0:HALF], nmax[0:HALF], nmax_parts[0:HALF, b.r % 2, :, 0, :], ALU.subtract).then_inc(nmr1, 1)

            def max_part1(b):
                wait(dve, nmr1, b)
                v.tensor_copy(nmax_parts[0:HALF, b.r % 2, :, 1, :], nmax_rest[0:HALF]).then_inc(nmp2, 1)

            def max_part2(b):
                wait(dve, nmp2, b)
                v.tensor_tensor(nmax_parts[0:HALF, b.r % 2, :, 2, :], nmax_rest[0:HALF], nmax_parts[0:HALF, b.r % 2, :, 1, :],
                                ALU.subtract).then_inc(nmp3, 1)

            def third_parts(b):
                wait(dve, part2, b)
                wait_dma(dve, third_out, b.lag(2))
                v.tensor_tensor(split(b.r % 2, 2), rest[:, b.r % 2], split(b.r % 2, 1),
                                ALU.subtract).then_inc(part3, 1)

            def first_rest(b):
                c = b.r % 2
                wait(dve, part1, b)
                wait(dve, part3, b.lag(2))
                v.tensor_tensor(rest[:, c], qk[:, c], split(c, 0), ALU.subtract).then_inc(rest1, 1)

            def tokens(b):
                wait(dve, conv_ps, b)
                wait(dve, base_part, b.lag(2), per=2)
                v.tensor_tensor(h[0:HALF, b.r % 2], ps[0:HALF, M1, 0:2 * D].rearrange("p (c u) -> p c u", c=2),
                                tok_b_sb[0:HALF, None, :].to_broadcast([HALF, 2, D]), ALU.add).then_inc(h_sb, 1)

            def token_stats(b):
                wait(dve, h_sb, b)
                for n in range(2):
                    v.bn_stats(stats[0:HALF, n, :], h[0:HALF, b.r % 2, n, :]).then_inc(st1, 1)

            def token_moments(b):
                c = b.r % 2
                wait(dve, st1, b, per=2)
                wait_apart(dve)
                v.bn_aggr(mv[0:HALF, c, 0, :], stats[0:HALF, 0, :])
                v.bn_aggr(mv[0:HALF, c, 1, :], stats[0:HALF, 1, :]).then_inc(mv_sb, 1)

            def normalise(b, n):
                c = b.r % 2
                if n == 0:
                    wait(dve, pool_rstd, b)
                    wait(dve, zT_ps, b.lag(2))
                v.tensor_scalar(z[0:HALF, c, n], h[0:HALF, c, n], mv[0:HALF, c, n, 0:1],
                                rstd[0:HALF, c, 2 + n:3 + n], ALU.subtract, ALU.mult).then_inc(z_sb, 1)

            def prob_sums(b):
                wait(dve, o_ps, b)
                o = ps[0:HALF, MID, :].rearrange("p (g c) -> p g c", c=32)
                v.reciprocal(rsum[0:HALF], o[:, :, HD]).then_inc(rsum_sb, 1)

            def divide(b):
                wait(dve, rsum_sb, b)
                wait(dve, cT_ps, b.lag(2))
                o = ps[0:HALF, MID, :].rearrange("p (g c) -> p g c", c=32)
                v.tensor_tensor(cn[0:HALF, b.r % 2].rearrange("p c (h d) -> p (c h) d", d=HD), o[:, :, 0:HD],
                                rsum[0:HALF, :, None].to_broadcast([HALF, 16, HD]), ALU.mult).then_inc(cn_sb, 1)

            def residual(b):
                wait(dve, proj_ps, b)
                wait(dve, base_sb, b)
                wait_dma(dve, scattered, b.lag(4), dmas=2)
                v.tensor_tensor(rec[0:HALF, b.r % 4, :, D:2 * D], ps[0:HALF, M0, 0:2 * D].rearrange("p (c u) -> p c u", c=2),
                                base[0:HALF, b.ap, :, :].rearrange("p a c u -> p (a c) u"), ALU.add).then_inc(h2_sb, 1)

            def residual_stats(b):
                wait(dve, h2_sb, b)
                for n in range(2):
                    v.bn_stats(stats2[0:HALF, n, :], rec[0:HALF, b.r % 4, n, D:2 * D]).then_inc(st2, 1)

            def residual_moments(b):
                c = b.r % 2
                wait(dve, st2, b, per=2)
                wait_apart(dve)
                v.bn_aggr(mv2[0:HALF, c, 0, :], stats2[0:HALF, 0, :])
                v.bn_aggr(mv2[0:HALF, c, 1, :], stats2[0:HALF, 1, :]).then_inc(mv2_sb, 1)

            def logit_bias(b):
                wait(dve, lg_ps, b)
                v.tensor_tensor(lg[0:HALF], ps[0:HALF, M1, 0:2 * D].rearrange("p (c u) -> p c u", c=2)[:, :, 0:E],
                                b_r_sb[0:HALF, None, :].to_broadcast([HALF, 2, E]), ALU.add).then_inc(lg_sb, 1)

            def logit_max(b):
                wait(dve, lg_sb, b)
                v.tensor_reduce(lmax[0:HALF], lg[0:HALF], AX.X, ALU.max).then_inc(lmax_sb, 1)

            def logit_diff(b):
                wait(dve, lmax_sb, b)
                wait(dve, lexp_sb, b.lag(2))
                v.tensor_tensor(ldiff[0:HALF, b.r % 2], lg[0:HALF], lmax[0:HALF, :, None].to_broadcast([HALF, 2, E]),
                                ALU.subtract).then_inc(ldiff_sb, 1)

            def hits(b):
                wait(dve, ldiff_sb, b)
                v.scalar_tensor_tensor(hit[0:HALF], ldiff[0:HALF, b.r % 2], 0.0,
                                       rank_weight[0:HALF, None, :].to_broadcast([HALF, 2, E]),
                                       ALU.is_equal, ALU.mult).then_inc(hit_sb, 1)

            def first_hit(b):
                wait(dve, hit_sb, b)
                v.tensor_reduce(first[0:HALF], hit[0:HALF], AX.X, ALU.max).then_inc(first_sb, 1)

            def one_expert(b):
                wait(dve, first_sb, b)
                wait(dve, rank_ps, b.lag(2))
                v.tensor_tensor(onehot[0:HALF, b.r % 2], hit[0:HALF], first[0:HALF, :, None].to_broadcast([HALF, 2, E]),
                                ALU.is_equal).then_inc(onehot_sb, 1)

            def record_id(b):
                v.tensor_copy(rec[0:HALF, b.r % 4, :, IDCOL].bitcast(I32), token[0:HALF]).then_inc(id_sb, 1)
                v.tensor_scalar(token[0:HALF], token[0:HALF], float(T), None, ALU.add).then_inc(token_moved, 1)

            def exp_sum(b):
                wait(dve, lexp_sb, b)
                v.tensor_reduce(lsum[0:HALF], lexp[0:HALF, b.r % 2], AX.X, ALU.add).then_inc(lsum_sb, 1)

            def record_gate(b):
                wait(dve, lsum_sb, b)
                v.reciprocal(rec[0:HALF, b.r % 4, :, GATE], lsum[0:HALF]).then_inc(gate_sb, 1)

            def positions(b):
                wait(dve, rank_ps, b)
                wait(dve, slots_moved, b.lag(1))
                v.tensor_tensor(pos[0:HALF], ps[0:HALF, M0, 0:2 * E].rearrange("p (c e) -> p c e", e=E),
                                next_slot[0:HALF, None, :].to_broadcast([HALF, 2, E]), ALU.add).then_inc(pos_sb, 1)

            def own_position(b):
                wait(dve, pos_sb, b)
                v.tensor_tensor(next_slot[0:HALF], ps[0:HALF, M0, 2 * E:3 * E], next_slot[0:HALF], ALU.add).then_inc(slots_moved, 1)
                v.tensor_tensor(pos_own[0:HALF], pos[0:HALF], onehot[0:HALF, b.r % 2], ALU.mult).then_inc(own_sb, 1)

            def slot_sum(b):
                wait(dve, own_sb, b)
                v.tensor_reduce(slot_f[0:HALF], pos_own[0:HALF], AX.X, ALU.add).then_inc(slotf_sb, 1)

            def slot_number(b):
                wait(dve, slotf_sb, b)
                v.tensor_copy(slot[0:HALF, b.r % 4, :], slot_f[0:HALF]).then_inc(slot_sb, 1)

            def step(i):
                j, n, u, r, q = i.lag(1), i.lag(2), i.lag(5), i.lag(6), i.lag(7)

                def turn(*work):
                    for stage, b, *rest_of in work:
                        if b.live():
                            stage(b, *rest_of)

                turn((row_max, n, 0), (positions, q), (own_position, q), (third_parts, j))
                turn((slot_sum, q), (row_max, n, 1), (slot_number, q))
                turn((tokens, i), (row_max, n, 2), (token_stats, i), (token_moments, i))
                if isinstance(i.k, int) and i.n == 0:
                    fold_biases()
                turn((row_max, n, 3))
                turn((prob_sums, u), (divide, u), (row_max, n, 4), (logit_bias, r), (normalise, i, 0), (logit_max, r),
                     (normalise, i, 1), (logit_diff, r))
                if isinstance(i.k, int) and i.n < 2:
                    v.memset(K[ROWS:MROWS, 2 * i.n:2 * i.n + 2], 1.0).then_inc(s_fill, 1)
                turn((row_max, n, 5), (hits, r), (record_id, r))
                turn((first_hit, r), (row_max, n, 6), (one_expert, r), (exp_sum, r))
                turn((residual, u), (row_max, n, 7), (residual_stats, u), (negate_max, n), (residual_moments, u), (max_part0, n),
                     (record_gate, r), (max_rest, n), (first_rest, i), (max_part1, n))
                turn((max_part2, n))

            pipeline(dve, step)

            chain = [0]

            def link(ins):
                chain[0] += 1
                ins.then_inc(s_plan2, 1)
                dve.wait_ge(s_plan2, chain[0])

            dve.wait_ge(slots_moved, NB)
            v.tensor_copy(tail_i[:], next_slot[0:1]).then_inc(s_tail, 1)
            link(v.tensor_tensor(count_i[:], next_slot[0:1], bin_start[0:1], ALU.subtract))
            link(v.tensor_scalar(tiles_i[:], count_i[:], 7, None, ALU.logical_shift_right))
            link(v.tensor_copy(tiles_f[:], tiles_i[:]))
            link(v.tensor_tensor_scan(tiles_end[:], one_e[:], tiles_f[:], 0.0, ALU.mult, ALU.add))
            v.tensor_scalar(skip[:], tiles_f[:], -1.0, float(BIN // 128), ALU.mult, ALU.add)
            link(v.tensor_tensor(passed[:], tiles_end[:, None, :].to_broadcast([1, TILES, E]),
                                 tile_no[:, :, None].to_broadcast([1, TILES, E]), ALU.is_le))
            link(v.tensor_tensor(skipped[:], passed[:], skip[:, None, :].to_broadcast([1, TILES, E]), ALU.mult))
            link(v.tensor_reduce(start_f[:], skipped[:], AX.X, ALU.add))
            link(v.tensor_tensor(row_f[:], tile_no[:], start_f[:], ALU.add))
            v.tensor_scalar(row_i[:], row_f[:], float(PAD_TILE), None, ALU.min).then_inc(s_plan, 1)
            link(v.tensor_reduce(expert_f[:], passed[:], AX.X, ALU.add))
            v.tensor_scalar(expert_i[:], expert_f[:], float(E - 1), None, ALU.min).then_inc(s_plan, 1)
            dve.wait_ge(b1T_ps, 1)
            v.tensor_copy(experts[:, :, 3 * D], ps[:, 0, 0:E]).then_inc(b1T_sb, 1)
            dve.wait_ge(s_plan, 2)
            dve.wait_ge(b1T_sb, 1)

            def step_b(t, e=None):
                if t.live(TILES):
                    wait(dve, y_half, t.lag(4), rows=TILES)
                    v.tensor_copy(expert[:, t.r % 4, :], experts[:, bass.ds(e, 1), :].rearrange("p a c -> p (a c)")).then_inc(expert_sb, 1)
                b = t.lag(3)
                if b.live(TILES):
                    wait(dve, y_ps, b, rows=TILES)
                    wait(dve, y_sb, b.lag(2), rows=TILES)
                    v.tensor_tensor(y_part[:, b.r % 2, :], ps[:, 6 + b.r % 2, 0:D],
                                    expert[:, b.r % 4, 2 * D:3 * D], ALU.add).then_inc(y_half, 1)
                b = t.lag(4)
                if b.live(TILES):
                    wait(dve, y_half, b, rows=TILES)
                    u = b.lag(Y_RING)
                    if not (isinstance(u.k, int) and u.n < 0):
                        wait_dma(dve, y_out, u, rows=TILES)
                    v.scalar_tensor_tensor(y[:, b.r % Y_RING, :], y_part[:, b.r % 2, :], tile_in[:, b.r % RING, GATE:GATE + 1],
                                           tile_in[:, b.r % RING, D:2 * D], ALU.mult, ALU.add).then_inc(y_sb, 1)

            pipeline_b(dve, step_b, upto=4, table=expert_i, max_val=E - 1)

        @block.tensor
        def _(pe):
            mm, tp = nc.tensor.matmul, nc.tensor.transpose
            def fold_biases():
                pe.wait_ge(loads, 16 * 7)
                pe.wait_ge(s_setup_pe, 3)
                pe.wait_ge(s_const, 1)
                mm(ps[:, 4, 0:1], w_raw[:, 0, :], beta_sb[:], start=True, stop=True)
                mm(ps[:, 4, 1:2], w_raw[:, 1, :], beta_sb[:], start=True, stop=True)
                mm(ps[:, 4, 2:3], w_qkv_sb[:, 2 * D:3 * D], beta_sb[:], start=True, stop=True).then_inc(s_ptail, 1)
                pe.wait_ge(s_setup_pe, 4)
                mm(ps[0:1, 5, 0:D], v_bias[:], w_out_sb[:], start=True, stop=True).then_inc(s_ptail, 1)
                pe.wait_ge(s_setup_pe, 5)
                mm(ps[:, 4, 0:D], ones_row[:], o_bias_row[:], start=True, stop=True).then_inc(s_ptail, 1)
                pe.wait_ge(s_setup, 1)

            def x_transpose(b):
                wait_dma(pe, x_in, b)
                wait(pe, v_sb, b.lag(2))
                wait(pe, z3T_sb, b.lag(7))
                for n in range(2):
                    last = tp(ps[:, M0, n * 128:(n + 1) * 128], xt[:, b.r % 4, n, :], ident[:])
                last.then_inc(xT_ps, 1)

            def conv(b, n):
                if n == 0:
                    wait(pe, xT_sb, b)
                    wait(pe, zT_sb, b.lag(1))
                for k in range(TAPS):
                    last = mm(ps[0:HALF, M1, n * D:(n + 1) * D], xT[:, b.r % 2, n * HALF + k:(n + 1) * HALF + k],
                              tok_w_sb[:, k, :], start=(k == 0), stop=(k == TAPS - 1))
                if n == 1:
                    last.then_inc(conv_ps, 1)

            def z_transpose(b):
                wait(pe, z_sb, b, per=2)
                wait(pe, lg_sb, b.lag(6))
                for n in range(2):
                    last = tp(ps[:, M1, n * HALF:(n + 1) * HALF], z[0:HALF, b.r % 2, n, :], ident[0:HALF, 0:HALF])
                last.then_inc(zT_ps, 1)

            def project_qk(b):
                wait(pe, zT_sb, b)
                wait(pe, cn_sb, b.lag(5))
                wait(pe, nmT_sb, b.lag(3))
                wait(pe, qk_sb, b.lag(1), per=2)
                for n, w in enumerate((w_q, w_k)):
                    last = mm(ps[:, MID, n * T:(n + 1) * T], w[:], zT[:, b.r % 2, :], start=True, stop=True)
                last.then_inc(qk_ps, 1)

            def project_v(b):
                wait(pe, slots_moved, b.lag(6))
                wait(pe, h2_sb, b.lag(5))
                wait(pe, xT_sb, b.lag(-1))
                for n in range(2):
                    last = mm(ps[0:HALF, M0, n * D:(n + 1) * D], zT[:, b.r % 2, n * HALF:(n + 1) * HALF], w_v[:],
                              start=True, stop=True)
                last.then_inc(v_ps, 1)

            def scores(b, hd):
                if hd == 0:
                    wait_dma(pe, stack_in, b, dmas=len(STACKS))
                c, bank = b.r % 4, NAT + hd % 2
                wait(pe, max_sb, b, per=HEADS, upto=hd - 1)
                mm(ps[0:HALF, bank, 0:HALF], Q[0:ROWS, c, hd, 0:HALF], K[0:ROWS, c, hd, 0:HALF], start=True, stop=False,
                   skip_group_check=True)
                mm(ps[0:HALF, bank, HALF:TRI], Q[0:ROWS, c, hd, HALF:T], K[0:ROWS, c, hd, :], start=False, stop=False,
                   skip_group_check=True)
                mm(bass_diag(ps[0:HALF, bank, 0:TRI]), ident_bf[0:HALF, 0:HALF], causal[0:HALF], start=False, stop=True,
                   skip_group_check=True).then_inc(nat_ps, 1)

            def scores_T(b, hd):
                if hd == 0:
                    wait_dma(pe, max_in, b)
                c, bank = b.r % 4, TRN + hd % 2
                wait(pe, exp_sb, b, per=HEADS, upto=hd - 1)
                mm(ps[0:HALF, bank, 0:T], K[0:MROWS, c, hd, 0:HALF], Q[0:MROWS, c, hd, :], start=True, stop=True,
                   skip_group_check=True)
                mm(ps[0:HALF, bank, T:TRI], K[0:MROWS, c, hd, HALF:T], Q[0:MROWS, c, hd, HALF:T], start=False, stop=True,
                   skip_group_check=True).then_inc(trn_ps, 1)

            def values(b, hd):
                if hd == 0:
                    wait(pe, oT_sb, b.lag(1))
                    wait(pe, v_sb, b)
                wait(pe, sel_sb, b, per=HEADS, upto=hd + 1)
                c, s, j = b.r % 4, hd // 4, 32 * (hd % 4)
                mm(ps[j:j + 32, AV, s * T:(s + 1) * T], V[0:HALF, c, 0, hd, :], P[0:HALF, hd, 0:T], start=True, stop=False,
                   skip_group_check=True)
                mm(ps[j:j + 32, AV, s * T + HALF:(s + 1) * T], V[0:HALF, c, 1, hd, :], P[0:HALF, hd, T:TRI],
                   start=False, stop=True, skip_group_check=True).then_inc(av_ps, 1)

            def max_transpose(b):
                wait(pe, nmp3, b)
                wait(pe, qk_sb, b.lag(-2), per=2)
                wait(pe, cn_sb, b.lag(3))
                wait(pe, nmT_sb, b.lag(1))
                for n in range(2):
                    last = tp(ps[0:PARTS * HEADS, MID, n * HALF // 2:(n + 1) * HALF // 2].bitcast(BF16),
                              nmax_parts[0:HALF, b.r % 2, n].rearrange("p s h -> p (s h)"), ident_bf[0:HALF, 0:HALF])
                last.then_inc(nmT_ps, 1)

            def heads_transpose(b):
                wait(pe, oT_sb, b)
                wait(pe, nmT_sb, b.lag(-2))
                wait(pe, cn_sb, b.lag(1))
                for n in range(2):
                    for s in range(2):
                        last = tp(ps[0:HALF, MID, (2 * n + s) * 128:(2 * n + s + 1) * 128],
                                  oT[:, s, n * HALF:(n + 1) * HALF], ident[:])
                last.then_inc(o_ps, 1)

            def c_transpose(b):
                wait(pe, cn_sb, b)
                wait(pe, xT_sb, b.lag(-6))
                wait(pe, z3T_sb, b.lag(1))
                for n in range(2):
                    last = tp(ps[:, M0, n * HALF:(n + 1) * HALF], cn[0:HALF, b.r % 2, n, :], ident[0:HALF, 0:HALF])
                last.then_inc(cT_ps, 1)

            def project_out(b):
                wait(pe, cT_sb, b)
                for n in range(2):
                    last = mm(ps[0:HALF, M0, n * D:(n + 1) * D], cT[:, b.r % 2, n * HALF:(n + 1) * HALF], w_out_sb[:],
                              start=True, stop=True)
                last.then_inc(proj_ps, 1)

            def z3_transpose(b):
                wait(pe, z3_sb, b, per=2)
                wait(pe, slots_moved, b.lag(1))
                wait(pe, v_sb, b.lag(-5))
                wait(pe, h2_sb, b)
                for n in range(2):
                    last = tp(ps[:, M0, n * HALF:(n + 1) * HALF], rec[0:HALF, b.r % 4, n, 0:D], ident[0:HALF, 0:HALF])
                last.then_inc(z3T_ps, 1)

            def logits(b):
                wait(pe, z3T_sb, b)
                wait(pe, h_sb, b.lag(-6))
                for n in range(2):
                    last = mm(ps[0:HALF, M1, n * D:(n + 1) * D], z3T[:, b.r % 2, n * HALF:(n + 1) * HALF], w_r_sb[:],
                              start=True, stop=True)
                last.then_inc(lg_ps, 1)

            def ranks(b):
                wait(pe, onehot_sb, b)
                wait(pe, h2_sb, b.lag(-1))
                oh = onehot[0:HALF, b.r % 2]
                mm(ps[0:HALF, M0, 0:2 * E], before[0:HALF], oh.rearrange("p c e -> p (c e)"), start=True, stop=False,
                   skip_group_check=True)
                mm(ps[0:HALF, M0, E:2 * E], ones_bf[0:HALF], oh[:, 0, :], start=False, stop=True, skip_group_check=True)
                for n in range(2):
                    last = mm(ps[0:HALF, M0, 2 * E:3 * E], ones_bf[0:HALF], oh[:, n, :], start=False, stop=(n == 1),
                              skip_group_check=True)
                last.then_inc(rank_ps, 1)

            pe.wait_ge(s_ident, 1)
            x_transpose(Row(0, 0))
            pe.wait_ge(tokeniser_in, 32)

            def step(i):
                j, n, s, b, u, r, q = i.lag(1), i.lag(2), i.lag(3), i.lag(4), i.lag(5), i.lag(6), i.lag(7)
                for hd in range(HEADS):
                    if b.live():
                        scores_T(b, hd)
                    if n.live():
                        scores(n, hd)
                    if hd == 0 and i.live():
                        conv(i, 0)
                    if hd == 1:
                        if i.live():
                            conv(i, 1)
                        if s.live():
                            max_transpose(s)
                        if isinstance(i.k, int) and i.n == 0:
                            fold_biases()
                    if hd == 2 and j.live():
                        project_v(j)
                    if hd == 3:
                        if u.live():
                            heads_transpose(u)
                        if r.live():
                            z3_transpose(r)
                    if hd == 4:
                        if i.lag(-1).live():
                            x_transpose(i.lag(-1))
                        if r.live():
                            logits(r)
                    if hd == 5 and u.live():
                        c_transpose(u)
                    if hd == 6 and i.live():
                        z_transpose(i)
                    if hd < 2:
                        if u.live():
                            values(u, hd + 6)
                    elif b.live():
                        values(b, hd - 2)
                    if hd == 0 and q.live():
                        ranks(q)
                    if hd == 6:
                        if u.live():
                            project_out(u)
                        if i.live():
                            project_qk(i)

            pipeline(pe, step)
            pe.wait_ge(loads, 16 * 11)
            tp(ps[:, 0, 0:E], b_1_rows[:], ident[0:E, 0:E]).then_inc(b1T_ps, 1)
            pe.wait_ge(b1T_sb, 1)

            def step_b(t):
                if t.live(TILES):
                    wait_dma(pe, t_in, t, rows=TILES)
                    wait(pe, tT_sb, t.lag(2), rows=TILES)
                    tp(ps[:, 0 + t.r % 2, 0:128], tile_in[:, t.r % RING, 0:D], ident[:]).then_inc(tT_ps, 1)
                b = t.lag(1)
                if b.live(TILES):
                    c = b.r % 2
                    wait(pe, expert_sb, b, rows=TILES)
                    wait(pe, tT_sb, b, rows=TILES)
                    wait(pe, hid_sb, b.lag(2), rows=TILES)
                    mm(ps[:, 2 + c, 0:128], expert[:, b.r % 4, 0:D], tT[:, c, :], start=True, stop=True).then_inc(hid_ps, 1)
                b = t.lag(2)
                if b.live(TILES):
                    c = b.r % 2
                    wait(pe, hid_sb, b, rows=TILES)
                    wait(pe, y_half, b.lag(2), rows=TILES)
                    mm(ps[:, 6 + c, 0:D], hidT[:, c, :], expert[:, b.r % 4, D:2 * D], start=True, stop=True).then_inc(y_ps, 1)

            pipeline_b(pe, step_b, upto=2)


_INS = ["x", "L0_tok_W", "L0_tok_b", "L0_attn_w_qkv", "L0_attn_w_out", "L0_attn_b_out", "L0_attn_gamma", "L0_attn_beta",
        "L0_ffn_Wr", "L0_ffn_br", "L0_ffn_W1", "L0_ffn_b1", "L0_ffn_W2", "L0_ffn_b2"]


def kernel(**inputs):
    import numpy as _np
    import concourse.bacc as _bacc
    from concourse import mybir as _mybir
    from concourse.bass_utils import run_bass_kernel_spmd as _run

    nc = _bacc.Bacc("TRN2", target_bir_lowering=False, num_devices=1)
    arrays, args = {}, []
    for name in _INS:
        a = _np.ascontiguousarray(inputs[name])
        arrays[f"in_{name}_dram"] = a
        args.append(nc.dram_tensor(f"in_{name}_dram", a.shape, _mybir.dt.from_np(a.dtype), kind="ExternalInput").ap())
    b, t, d = inputs["x"].shape
    taps = inputs["L0_tok_W"].shape[0] // d
    shape = (b, t - taps + 1, d)
    args.append(nc.dram_tensor("out_0_dram", shape, _mybir.dt.float32, kind="ExternalOutput").ap())
    build(nc, *args)
    r = _run(nc, [arrays], core_ids=[0])
    return r.results[0]["out_0_dram"]
```
